# Optimizing a Trainium2 kernel written in Bass

```python
import numpy as np
import jax
import jax.numpy as jnp

def _softmax(x, axis=-1):
    return jax.nn.softmax(x, axis=axis)

def _gelu(x):
    return jax.nn.gelu(x, approximate=True)

def _silu(x):
    return jax.nn.silu(x)

def _sigmoid(x):
    return jax.nn.sigmoid(x)

def _layernorm(x, axis=-1, eps=1e-05):
    m = jnp.mean(x, axis=axis, keepdims=True)
    v = jnp.var(x, axis=axis, keepdims=True)
    return (x - m) / jnp.sqrt(v + eps)

def _scatter_add(tgt, idx, src, axis=0):
    return tgt.at[idx].add(src)

def _segment_sum(src, seg, n):
    return jax.ops.segment_sum(src, seg, n)
kernel_name = 'mk_flamingo_gated_d1_seqx_r8_c8f56e'

def setup_inputs(seed: int=0):
    np.random.seed(seed)
    _w = jnp.asarray

    def _rec_inputs():
        import jax
        import jax.numpy as jnp
        _rk = jax.random.key(seed)
        x = 7.22e-05 + 1 * jax.random.normal(jax.random.fold_in(_rk, 1), (4, 512, 128), jnp.float32)
        _lenS = 512 - jax.random.randint(jax.random.fold_in(_rk, 7), (4,), 0, max(1, 512 // 4) + 1, jnp.int32)
        _lenS2 = 77 - jax.random.randint(jax.random.fold_in(_rk, 8), (4,), 0, max(1, 77 // 4) + 1, jnp.int32)
        _ctx_1024P = jax.random.normal(jax.random.fold_in(_rk, 11), (4, 16, 128), jnp.float32)
        _ctx_1024c = jax.random.dirichlet(jax.random.fold_in(_rk, 511), 0.3 * jnp.ones((16,), jnp.float32), (4, 77))
        _ctx_1024t = jnp.einsum('bsk,bkd->bsd', _ctx_1024c, _ctx_1024P)
        _ctx_1024t = _ctx_1024t * jax.lax.rsqrt(jnp.mean(jnp.square(_ctx_1024t)) + 1e-12) * 0.953939
        ctx_1024 = 4.13588e-05 + 0.999923 * (_ctx_1024t + 0.3 * jax.random.normal(jax.random.fold_in(_rk, 611), (4, 77, 128), jnp.float32))
        _g = jax.random.normal(jax.random.fold_in(_rk, 9001), (2, 1), jnp.float32)
        _g = jnp.sign(_g) * jnp.maximum(jnp.abs(_g), 1.0) + (_g == 0) * 1.0
        g_xattn = _g[0]
        g_ffn = _g[1]
        return (x, ctx_1024, g_xattn, g_ffn)
    x, ctx_1024, g_xattn, g_ffn = _rec_inputs()

    def _L0_xattn_setup():
        import jax, jax.numpy as jnp
        import numpy as np
        C = 128
        B, SQ, SKV = (4, 256, 256)
        key = jax.random.key(seed)
        ks = jax.random.split(key, 10)
        s = 1.0 / np.sqrt(C)
        return {'x': jax.random.normal(ks[0], (B, SQ, C), jnp.float32), 'content_embeddings': jax.random.normal(ks[1], (B, SKV, C), jnp.float32), 'Wq': jax.random.normal(ks[2], (C, C), jnp.float32) * s, 'bq': jnp.zeros((C,), jnp.float32), 'Wk': jax.random.normal(ks[3], (C, C), jnp.float32) * s, 'bk': jnp.zeros((C,), jnp.float32), 'Wv': jax.random.normal(ks[4], (C, C), jnp.float32) * s, 'bv': jnp.zeros((C,), jnp.float32), 'Wo': jax.random.normal(ks[5], (C, C), jnp.float32) * s, 'bo': jnp.zeros((C,), jnp.float32)}
    _L0_xattn_all = _L0_xattn_setup()
    _L0_xattn_in = {k: v for k, v in _L0_xattn_all.items() if k in ('Wq', 'bq', 'Wk', 'bk', 'Wv', 'bv', 'Wo', 'bo')}
    del _L0_xattn_all

    def _L0_ffn_setup():
        import jax, jax.numpy as jnp
        import numpy as np
        DIM = 128
        DEPTH = 6
        HEADS = 16
        DIM_HEAD = 64
        WINDOW = 32
        INNER = HEADS * DIM_HEAD
        DIM_INNER = int(DIM * 4 * 2 / 3)
        QK_SCALE = 8.0

        def shift_tokens(t):
            a, s = jnp.split(t, 2, -1)
            s = jnp.pad(s, ((0, 0), (1, 0), (0, 0)))[:, :-1]
            return jnp.concatenate([a, s], -1)

        def l2norm(t):
            return t / jnp.maximum(jnp.linalg.norm(t, axis=-1, keepdims=True), 1e-12)

        def rotate_half(x):
            x1, x2 = jnp.split(x, 2, -1)
            return jnp.concatenate([-x2, x1], -1)

        def rotary_tables(n):
            half = jnp.arange(0, DIM_HEAD, 2, dtype=jnp.float32)
            inv_freq = 1.0 / 10000.0 ** (half / DIM_HEAD)
            t = jnp.arange(n, dtype=jnp.float32)
            freqs = t[:, None] * inv_freq[None, :]
            freqs = jnp.concatenate([freqs, freqs], -1)
            base_scale = (half + 0.4 * DIM_HEAD) / (1.4 * DIM_HEAD)
            power = (t - n // 2) / (WINDOW // 2)
            scale = base_scale[None, :] ** power[:, None]
            scale = jnp.concatenate([scale, scale], -1)
            return (freqs, scale)

        def local_attention(q, k, v):
            b, h, n, d = q.shape
            w = WINDOW
            nw = n // w
            bq = q.reshape(b, h, nw, w, d)
            bk = k.reshape(b, h, nw, w, d)
            bv = v.reshape(b, h, nw, w, d)

            def look(t):
                p = jnp.pad(t, ((0, 0), (0, 0), (1, 0), (0, 0), (0, 0)))
                return jnp.concatenate([p[:, :, :nw], p[:, :, 1:]], axis=3)
            bk2, bv2 = (look(bk), look(bv))
            seq = jnp.arange(n).reshape(nw, w)
            seq_p = jnp.pad(seq, ((1, 0), (0, 0)), constant_values=-1)
            jt = jnp.concatenate([seq_p[:nw], seq_p[1:]], axis=1)
            it = seq[:, :, None]
            jb = jt[:, None, :]
            mask = (it < jb) | (it > jb + w) | (jb == -1)
            sim = jnp.einsum('bhwie,bhwje->bhwij', bq, bk2) * QK_SCALE
            sim = jnp.where(mask, -jnp.finfo(sim.dtype).max, sim)
            attn = jax.nn.softmax(sim, -1)
            out = jnp.einsum('bhwij,bhwje->bhwie', attn, bv2)
            return out.reshape(b, h, n, d)

        def attn_layer(x, Wqkv, qs, ksc, Wo):
            b, n, _ = x.shape
            qkv = x @ Wqkv
            q, k, v = jnp.split(qkv, 3, -1)
            sh = lambda t: t.reshape(b, n, HEADS, DIM_HEAD).transpose(0, 2, 1, 3)
            q, k, v = (sh(q), sh(k), sh(v))
            q = l2norm(q) * qs
            k = l2norm(k) * ksc
            freqs, scale = rotary_tables(n)
            cos, sin = (jnp.cos(freqs), jnp.sin(freqs))
            q = q * cos * scale + rotate_half(q) * sin * scale
            inv = 1.0 / scale
            k = k * cos * inv + rotate_half(k) * sin * inv
            out = local_attention(q, k, v)
            out = out.transpose(0, 2, 1, 3).reshape(b, n, INNER)
            return out @ Wo

        def ffn_layer(x, g, bln, W1, b1, W2, b2):
            mu = x.mean(-1, keepdims=True)
            var = ((x - mu) ** 2).mean(-1, keepdims=True)
            xn = (x - mu) / jnp.sqrt(var + 1e-05) * g + bln
            hg = xn @ W1 + b1
            a, gate = jnp.split(hg, 2, -1)
            return a * jax.nn.gelu(gate, approximate=False) @ W2 + b2
        key = jax.random.key(seed)
        ks = jax.random.split(key, 8)
        B, N = (2, 256)
        init = lambda k, shape: jax.random.normal(k, shape, jnp.float32) * 0.02
        return {'x': jax.random.normal(ks[0], (B, N, DIM), jnp.float32), 'Wqkv': init(ks[1], (DEPTH, DIM, 3 * INNER)), 'q_scale': jnp.ones((DEPTH, DIM_HEAD), jnp.float32), 'k_scale': jnp.ones((DEPTH, DIM_HEAD), jnp.float32), 'Wo': init(ks[2], (DEPTH, INNER, DIM)), 'ln_g': jnp.ones((DEPTH, DIM), jnp.float32), 'ln_b': jnp.zeros((DEPTH, DIM), jnp.float32), 'W1': init(ks[3], (DEPTH, DIM, 2 * DIM_INNER)), 'b1': jnp.zeros((DEPTH, 2 * DIM_INNER), jnp.float32), 'W2': init(ks[4], (DEPTH, DIM_INNER, DIM)), 'b2': jnp.zeros((DEPTH, DIM), jnp.float32)}
    _L0_ffn_all = _L0_ffn_setup()
    _L0_ffn_in = {k: v for k, v in _L0_ffn_all.items() if k in ('Wqkv', 'q_scale', 'k_scale', 'Wo', 'ln_g', 'ln_b', 'W1', 'b1', 'W2', 'b2')}
    del _L0_ffn_all
    return {'x': x, 'ctx_1024': ctx_1024, 'g_xattn': g_xattn, 'g_ffn': g_ffn, 'L0_xattn_Wq': _L0_xattn_in['Wq'], 'L0_xattn_bq': _L0_xattn_in['bq'], 'L0_xattn_Wk': _L0_xattn_in['Wk'], 'L0_xattn_bk': _L0_xattn_in['bk'], 'L0_xattn_Wv': _L0_xattn_in['Wv'], 'L0_xattn_bv': _L0_xattn_in['bv'], 'L0_xattn_Wo': _L0_xattn_in['Wo'], 'L0_xattn_bo': _L0_xattn_in['bo'], 'L0_ffn_Wqkv': _L0_ffn_in['Wqkv'], 'L0_ffn_q_scale': _L0_ffn_in['q_scale'], 'L0_ffn_k_scale': _L0_ffn_in['k_scale'], 'L0_ffn_Wo': _L0_ffn_in['Wo'], 'L0_ffn_ln_g': _L0_ffn_in['ln_g'], 'L0_ffn_ln_b': _L0_ffn_in['ln_b'], 'L0_ffn_W1': _L0_ffn_in['W1'], 'L0_ffn_b1': _L0_ffn_in['b1'], 'L0_ffn_W2': _L0_ffn_in['W2'], 'L0_ffn_b2': _L0_ffn_in['b2']}

def reference(x, ctx_1024, g_xattn, g_ffn, L0_xattn_Wq, L0_xattn_bq, L0_xattn_Wk, L0_xattn_bk, L0_xattn_Wv, L0_xattn_bv, L0_xattn_Wo, L0_xattn_bo, L0_ffn_Wqkv, L0_ffn_q_scale, L0_ffn_k_scale, L0_ffn_Wo, L0_ffn_ln_g, L0_ffn_ln_b, L0_ffn_W1, L0_ffn_b1, L0_ffn_W2, L0_ffn_b2):
    import jax
    import jax.numpy as jnp

    def _L0_xattn_ref(x, content_embeddings, Wq, bq, Wk, bk, Wv, bv, Wo, bo):
        import jax, jax.numpy as jnp
        import numpy as np
        C = 128
        B, SQ, SKV = (4, 256, 256)
        queries = x @ Wq.T + bq
        keys = content_embeddings @ Wk.T + bk
        values = content_embeddings @ Wv.T + bv
        scale = 1.0 / jnp.sqrt(jnp.asarray(C, x.dtype))
        scores = jnp.einsum('bqc,bkc->bqk', queries, keys) * scale
        attn = jax.nn.softmax(scores, axis=-1)
        attended = jnp.einsum('bqk,bkc->bqc', attn, values)
        out = x + attended
        return out @ Wo.T + bo

    def _L0_ffn_ref(x, Wqkv, q_scale, k_scale, Wo, ln_g, ln_b, W1, b1, W2, b2):
        import jax, jax.numpy as jnp
        import numpy as np
        DIM = 128
        DEPTH = 6
        HEADS = 16
        DIM_HEAD = 64
        WINDOW = 32
        INNER = HEADS * DIM_HEAD
        DIM_INNER = int(DIM * 4 * 2 / 3)
        QK_SCALE = 8.0

        def shift_tokens(t):
            a, s = jnp.split(t, 2, -1)
            s = jnp.pad(s, ((0, 0), (1, 0), (0, 0)))[:, :-1]
            return jnp.concatenate([a, s], -1)

        def l2norm(t):
            return t / jnp.maximum(jnp.linalg.norm(t, axis=-1, keepdims=True), 1e-12)

        def rotate_half(x):
            x1, x2 = jnp.split(x, 2, -1)
            return jnp.concatenate([-x2, x1], -1)

        def rotary_tables(n):
            half = jnp.arange(0, DIM_HEAD, 2, dtype=jnp.float32)
            inv_freq = 1.0 / 10000.0 ** (half / DIM_HEAD)
            t = jnp.arange(n, dtype=jnp.float32)
            freqs = t[:, None] * inv_freq[None, :]
            freqs = jnp.concatenate([freqs, freqs], -1)
            base_scale = (half + 0.4 * DIM_HEAD) / (1.4 * DIM_HEAD)
            power = (t - n // 2) / (WINDOW // 2)
            scale = base_scale[None, :] ** power[:, None]
            scale = jnp.concatenate([scale, scale], -1)
            return (freqs, scale)

        def local_attention(q, k, v):
            b, h, n, d = q.shape
            w = WINDOW
            nw = n // w
            bq = q.reshape(b, h, nw, w, d)
            bk = k.reshape(b, h, nw, w, d)
            bv = v.reshape(b, h, nw, w, d)

            def look(t):
                p = jnp.pad(t, ((0, 0), (0, 0), (1, 0), (0, 0), (0, 0)))
                return jnp.concatenate([p[:, :, :nw], p[:, :, 1:]], axis=3)
            bk2, bv2 = (look(bk), look(bv))
            seq = jnp.arange(n).reshape(nw, w)
            seq_p = jnp.pad(seq, ((1, 0), (0, 0)), constant_values=-1)
            jt = jnp.concatenate([seq_p[:nw], seq_p[1:]], axis=1)
            it = seq[:, :, None]
            jb = jt[:, None, :]
            mask = (it < jb) | (it > jb + w) | (jb == -1)
            sim = jnp.einsum('bhwie,bhwje->bhwij', bq, bk2) * QK_SCALE
            sim = jnp.where(mask, -jnp.finfo(sim.dtype).max, sim)
            attn = jax.nn.softmax(sim, -1)
            out = jnp.einsum('bhwij,bhwje->bhwie', attn, bv2)
            return out.reshape(b, h, n, d)

        def attn_layer(x, Wqkv, qs, ksc, Wo):
            b, n, _ = x.shape
            qkv = x @ Wqkv
            q, k, v = jnp.split(qkv, 3, -1)
            sh = lambda t: t.reshape(b, n, HEADS, DIM_HEAD).transpose(0, 2, 1, 3)
            q, k, v = (sh(q), sh(k), sh(v))
            q = l2norm(q) * qs
            k = l2norm(k) * ksc
            freqs, scale = rotary_tables(n)
            cos, sin = (jnp.cos(freqs), jnp.sin(freqs))
            q = q * cos * scale + rotate_half(q) * sin * scale
            inv = 1.0 / scale
            k = k * cos * inv + rotate_half(k) * sin * inv
            out = local_attention(q, k, v)
            out = out.transpose(0, 2, 1, 3).reshape(b, n, INNER)
            return out @ Wo

        def ffn_layer(x, g, bln, W1, b1, W2, b2):
            mu = x.mean(-1, keepdims=True)
            var = ((x - mu) ** 2).mean(-1, keepdims=True)
            xn = (x - mu) / jnp.sqrt(var + 1e-05) * g + bln
            hg = xn @ W1 + b1
            a, gate = jnp.split(hg, 2, -1)
            return a * jax.nn.gelu(gate, approximate=False) @ W2 + b2
        for i in range(DEPTH):
            x = attn_layer(shift_tokens(x), Wqkv[i], q_scale[i], k_scale[i], Wo[i]) + x
            x = ffn_layer(shift_tokens(x), ln_g[i], ln_b[i], W1[i], b1[i], W2[i], b2[i]) + x
        return x
    x = x + jnp.tanh(g_xattn[0]) * _L0_xattn_ref(_layernorm(x, axis=-1), ctx_1024, L0_xattn_Wq, L0_xattn_bq, L0_xattn_Wk, L0_xattn_bk, L0_xattn_Wv, L0_xattn_bv, L0_xattn_Wo, L0_xattn_bo)
    x = x + jnp.tanh(g_ffn[0]) * _L0_ffn_ref(_layernorm(x, axis=-1), L0_ffn_Wqkv, L0_ffn_q_scale, L0_ffn_k_scale, L0_ffn_Wo, L0_ffn_ln_g, L0_ffn_ln_b, L0_ffn_W1, L0_ffn_b1, L0_ffn_W2, L0_ffn_b2)
    return x

_drawn_inputs = setup_inputs


def setup_inputs(seed=0):
    import zlib

    import numpy as np

    out = dict(_drawn_inputs(seed))
    spreads = {'L0_xattn_bq': (0.0, 0.421),
     'L0_xattn_bk': (0.0, 0.8),
     'L0_xattn_bv': (0.0, 0.1),
     'L0_xattn_bo': (0.0, 0.1),
     'L0_ffn_q_scale': (1.0, 0.6),
     'L0_ffn_k_scale': (1.0, 0.6),
     'L0_ffn_ln_g': (1.0, 0.6),
     'L0_ffn_ln_b': (0.0, 0.8),
     'L0_ffn_b1': (0.0, 0.1),
     'L0_ffn_b2': (0.0, 0.1)}
    factors = {}
    for name, (base, spread) in spreads.items():
        noise = np.random.default_rng([zlib.crc32(name.encode()), seed]).standard_normal(out[name].shape)
        drawn = base * np.exp(spread * noise) if base else spread * noise
        out[name] = jnp.asarray(drawn.astype(out[name].dtype))
    for name, factor in factors.items():
        out[name] = (out[name] * factor).astype(out[name].dtype)
    return out
```

```python
from contextlib import ExitStack

import numpy as np

import concourse.bass as bass
from concourse import mybir

F32 = mybir.dt.float32
BF16 = mybir.dt.bfloat16
ALU = mybir.AluOpType
ACT = mybir.ActivationFunctionType
AX = mybir.AxisListType

P = 128
B, N, C = 4, 512, 128
CTX = 77
DEPTH, HEADS, DH, WIN = 6, 16, 64, 32
INNER = HEADS * DH
DFF = 341
TPG = N // P
GROUPS = DEPTH * B
HALVES = 2
UPG = TPG * HALVES
UNITS = GROUPS * UPG
HU = HEADS // HALVES
HP = HU // 2
UW = HU * DH
NW = P // WIN
BLK = [(0, 128), (128, 128), (256, DFF - 256)]
LN_EPS = 1e-5

TURNS = ["y2", "shift_att", "y3", "shift_ffn", "y0", "ln_t", "gate0", "gate1", "gate2", "y1", "x_t", "down"]
FIRST_TURNS = ["shift_att", "y0", "y1", "x_t"]
LAST_TURNS = ["y2", "y3", "shift_ffn", "ln_t", "gate0", "gate1", "gate2", "down"]


def turn(g, name):
    if isinstance(g, int) and g == 0:
        return FIRST_TURNS.index(name) + 1
    lacking = len(TURNS) - len(FIRST_TURNS)
    order = LAST_TURNS if isinstance(g, int) and g == GROUPS else TURNS
    return len(TURNS) * g - lacking + order.index(name) + 1


def constants():
    f = np.float32
    half = np.arange(0, DH, 2, dtype=f)
    inv_freq = (f(1.0) / f(10000.0) ** (half / f(DH))).astype(f)
    t = np.arange(N, dtype=f)
    freqs = t[:, None] * inv_freq[None, :]
    base = (half + f(0.4 * DH)) / f(1.4 * DH)
    power = (t - f(N // 2)) / f(WIN // 2)
    scale = base[None, :] ** power[:, None]
    inv = f(1.0) / scale
    cos, sin = np.cos(freqs), np.sin(freqs)
    both = lambda a, b: np.concatenate([a, b], 1)
    qk_scale = f(8.0)
    tables = np.concatenate([
        both(cos * scale, cos * scale) * qk_scale, both(-sin * scale, sin * scale) * qk_scale,
        both(cos * inv, cos * inv), both(-sin * inv, sin * inv)], 1).astype(f)
    rope = tables.reshape(TPG, P, 4 * DH).transpose(1, 0, 2)
    ident = np.eye(P, dtype=f)
    down1 = np.eye(P, k=1, dtype=f)
    wrap = np.zeros((P, P), f)
    wrap[P - 1, 0] = 1.0
    i = np.arange(P)[:, None] % WIN
    j = np.arange(2 * WIN)[None, :]
    seen = (j >= i) & (j <= i + WIN)
    first = seen & ((np.arange(P)[:, None] >= WIN) | (j >= WIN))
    mask = np.where(np.stack([first, seen], 1), f(0.0), f(-3.0e38)).astype(f)
    return (np.ascontiguousarray(rope), np.concatenate([ident, down1, wrap], 1),
            np.ascontiguousarray(mask))


def build(nc, x_in, ctx_in, g_xattn, g_ffn, Wq, bq, Wk, bk, Wv, bv, Wo_x, bo, Wqkv, q_scale, k_scale,
          Wo, ln_g, ln_b, W1, b1, W2, b2, rope_in, mats_in, mask_in, out):
    ctx = ExitStack()
    with ctx:
        def sb(name, shape, dt=F32):
            return ctx.enter_context(nc.sbuf_tensor(name, shape, dt))

        def sem(name):
            return ctx.enter_context(nc.semaphore(name))

        ps = [ctx.enter_context(nc.psum_tensor(f"bank{i}", [P, 512], F32)) for i in range(8)]
        QKV_BANKS, QT_BANK, KT_BANK, SC_BANK, PT_BANK, PV_BANK, SHARED = ps[0:2], ps[2], ps[3], ps[4], ps[5], ps[6], ps[7]

        mats = sb("mats", [P, 3 * P])
        ident, down1, wrap = mats[:, 0:P], mats[:, P:2 * P], mats[:, 2 * P:3 * P]
        mask_f = sb("mask_f", [P, 2, 2 * WIN])
        mask_b = sb("mask_b", [P, 2, 2 * WIN], BF16)
        ident_b = sb("ident_b", [P, P], BF16)
        rope = sb("rope", [P, TPG, 4 * DH])
        scales = sb("scales", [P, DEPTH, 4 * DH])
        tables = sb("tables", [P, 2, TPG, 4 * DH])
        wqkv = sb("wqkv", [P, 2, 3 * INNER])
        wo = sb("wo", [P, 2, INNER // P, C])
        w1 = sb("w1", [P, 2 * DFF])
        w2 = sb("w2", [P, len(BLK), C])
        b2r = sb("b2r", [P, DEPTH, C])
        cols = sb("cols", [P, DEPTH, 8])
        cur = sb("cur", [P, 8])
        x1 = sb("x1", [P, B * TPG, C])
        x = sb("x", [P, B * TPG, C])
        xa = sb("xa", [P, TPG, C])
        xsT = sb("xsT", [P, N])
        xf = sb("xf", [P, TPG, C])
        xn = sb("xn", [P, TPG, C])
        xnT = sb("xnT", [P, N])
        uT = sb("uT", [P, len(BLK), N])
        stats = sb("stats", [P, TPG, 6])
        mv = sb("mv", [P, TPG, 2])
        vare = sb("vare", [P, TPG])
        rstd = sb("rstd", [P, TPG])
        minus_half = sb("minus_half", [P, 2 * HU])
        qk = sb("qk", [P, 2, 2 * UW])
        sq = sb("sq", [P, 2 * UW])
        ra = sb("ra", [P, 2 * UW])
        rb = sb("rb", [P, 2 * UW])
        qkn = sb("qkn", [P, 2, 2 * UW])
        ss = sb("ss", [P, 2, 2 * HU])
        ssm = sb("ssm", [P, 2 * HU])
        rn = sb("rn", [P, 2, 2 * HU])
        qT = sb("qT", [P, 2, HP, P])
        kB = sb("kB", [P, HALVES * HP, 2, WIN + N])
        vs = sb("vs", [P, 4, 2, HP, DH])
        vw = sb("vw", [P, 2, NW, 2, HP * DH])
        pr = sb("pr", [P, 2, UW])
        pT = sb("pT", [P, 2, HP, P])
        o = sb("o", [P, UW])
        oT = sb("oT", [P, 2, INNER // P, P])
        mx = sb("mx", [P, HU])
        rs = sb("rs", [P, HU])
        rr = sb("rr", [P, 2, HU])
        free = vw[:, :, :, :, :].rearrange("p k w h n -> p (k w h n)")

        def take(start, groups, width):
            return free[:, start:start + groups * width].rearrange("p (a c) -> p a c", c=width)

        wx_in, wxT = take(0, 4, C), take(512, 4, C)
        ctx_sb, vx = take(1024, B, C)[0:CTX], take(1536, B, C)[0:CTX]
        ctxT, kxT = take(2048, B, CTX), take(2560, B, CTX)
        bcol = sb("bcol", [P, 2])
        brow = sb("brow", [1, 2, C])
        ones = sb("ones", [1, P])
        gcol = sb("gcol", [P, 2])
        tg = sb("tg", [P, 2])
        mx4 = sb("mx4", [P, TPG])
        rs4 = sb("rs4", [P, TPG])
        rr4 = sb("rr4", [P, TPG])

        x_dma = sem("x_dma")
        cst_dma = sem("cst_dma")
        small_dma = sem("small_dma")
        wx_dma = sem("wx_dma")
        w_dma = sem("w_dma")
        w1_dma = sem("w1_dma")
        w2_dma = sem("w2_dma")
        cols_dma = sem("cols_dma")
        out_dma = sem("out_dma")
        cst_ready = sem("cst_ready")
        settled = sem("settled")
        zero_ready = sem("zero_ready")
        vw_zero = sem("vw_zero")
        tanh_ready = sem("tanh_ready")
        table_ready = sem("table_ready")
        wxT_mm = sem("wxT_mm")
        wxT_ev = sem("wxT_ev")
        ctxT_mm = sem("ctxT_mm")
        ctxT_ev = sem("ctxT_ev")
        kx_mm = sem("kx_mm")
        kx_ev = sem("kx_ev")
        vx_mm = sem("vx_mm")
        vx_ev = sem("vx_ev")
        a_stat = sem("a_stat")
        a_rstd = sem("a_rstd")
        a_xn = sem("a_xn")
        a_xnT = sem("a_xnT")
        a_xnTev = sem("a_xnTev")
        a_q = sem("a_q")
        a_qev = sem("a_qev")
        a_sc = sem("a_sc")
        a_mx = sem("a_mx")
        a_sub = sem("a_sub")
        a_exp = sem("a_exp")
        a_sum = sem("a_sum")
        a_rec = sem("a_rec")
        a_pn = sem("a_pn")
        a_pT = sem("a_pT")
        a_pTev = sem("a_pTev")
        a_att = sem("a_att")
        a_res = sem("a_res")
        a_rT = sem("a_rT")
        a_rTev = sem("a_rTev")
        a_y = sem("a_y")
        a_x1 = sem("a_x1")
        b_stat = sem("b_stat")
        b_rstd = sem("b_rstd")
        b_x = sem("b_x")
        p_shift = sem("p_shift")
        p_up = sem("p_up")
        p_low = sem("p_low")
        p_xT = sem("p_xT")
        qkv_mm = sem("qkv_mm")
        qkv_ev = sem("qkv_ev")
        sq_done = sem("sq_done")
        cos_done = sem("cos_done")
        sin_done = sem("sin_done")
        ss_done = sem("ss_done")
        ssm_done = sem("ssm_done")
        rn_done = sem("rn_done")
        rot_done = sem("rot_done")
        qkn_done = sem("qkn_done")
        qT_mm = sem("qT_mm")
        kT_mm = sem("kT_mm")
        qT_ev = sem("qT_ev")
        kT_ev = sem("kT_ev")
        score_mm = sem("score_mm")
        max_done = sem("max_done")
        sub_done = sem("sub_done")
        exp_done = sem("exp_done")
        sum_done = sem("sum_done")
        rec_done = sem("rec_done")
        pT_mm = sem("pT_mm")
        pT_ev = sem("pT_ev")
        pv_mm = sem("pv_mm")
        o_done = sem("o_done")
        oT_mm = sem("oT_mm")
        oT_ev = sem("oT_ev")
        att_res = sem("att_res")
        turn_mm = sem("turn_mm")
        turn_read = sem("turn_read")
        xa_low = sem("xa_low")
        xsT_ev = sem("xsT_ev")
        xf_low = sem("xf_low")
        f_stat = sem("f_stat")
        f_aggr = sem("f_aggr")
        f_var = sem("f_var")
        f_rstd = sem("f_rstd")
        f_xn = sem("f_xn")
        b2_done = sem("b2_done")
        cur_done = sem("cur_done")
        xnT_done = sem("xnT_done")
        a_mm = sem("a_mm")
        u_done = sem("u_done")
        fin = sem("fin")
        vw_dma = [sem(f"vw_dma{i}") for i in range(2)]

        def past(count):
            return max(count, 0) if isinstance(count, int) else count

        def ahead(count):
            return count + 1

        def settle(eng):
            eng.sem_inc(settled, 1)

        def alive(g, s, lag):
            if isinstance(g, int) and g == 0:
                return s >= lag
            if isinstance(g, int) and g == GROUPS:
                return s < lag
            return True

        def has_group(g, back):
            if isinstance(g, int) and g == 0:
                return back == 0
            if isinstance(g, int) and g == GROUPS:
                return back == 1
            return True

        def heads(ap, d=DH):
            return ap.rearrange("p (h d) -> p h d", d=d)

        def spread(ap, n):
            return ap.unsqueeze(2).to_broadcast([P, ap.shape[1], n])

        def vw_count(g, s):
            per_unit = 2 * (NW + 1)
            per_group = per_unit * TPG - 2
            return 16 * (per_group * g + per_unit * (s // HALVES + 1) - 2)

        block = ctx.enter_context(nc.Block())

        @block.sync
        def _(sp):
            xt = x_in.rearrange("b (t p) c -> p (b t) c", p=P)
            sp.dma_start(x1[:, 0:TPG, :], xt[:, 0:TPG, :]).then_inc(x_dma, 16)
            sp.dma_start(mats[:, :], mats_in).then_inc(cst_dma, 16)
            sp.dma_start(mask_f[:, :, :], mask_in).then_inc(cst_dma, 16)
            sp.dma_start(ctx_sb[:, :, :], ctx_in.rearrange("b s c -> s b c")).then_inc(wx_dma, 16)
            for i, w in enumerate((Wq, Wk, Wv, Wo_x)):
                sp.dma_start(wx_in[:, i, :], w).then_inc(wx_dma, 16)
            sp.dma_start(bcol[:, 0:1], bq.unsqueeze(1)).then_inc(small_dma, 16)
            sp.dma_start(bcol[:, 1:2], bk.unsqueeze(1)).then_inc(small_dma, 16)
            sp.dma_start(brow[:, 0, :], bv.unsqueeze(0)).then_inc(small_dma, 16)
            sp.dma_start(brow[:, 1, :], bo.unsqueeze(0)).then_inc(small_dma, 16)
            sp.dma_start(gcol[:, 0:1], g_xattn.unsqueeze(0).to_broadcast([P, 1])).then_inc(small_dma, 16)
            sp.dma_start(gcol[:, 1:2], g_ffn.unsqueeze(0).to_broadcast([P, 1])).then_inc(small_dma, 16)
            sp.dma_start(x1[:, TPG:, :], xt[:, TPG:, :]).then_inc(x_dma, 16)
            sp.dma_start(rope[:, :, :], rope_in).then_inc(cst_dma, 16)
            h = DH // 2
            for i, s in enumerate((q_scale, k_scale)):
                for dst, src in ((0, 0), (DH, h), (DH + h, 0)):
                    n = DH if dst == 0 else h
                    sp.dma_start(scales[:, :, 2 * DH * i + dst:2 * DH * i + dst + n],
                                 s[:, src:src + n].unsqueeze(0).to_broadcast([P, DEPTH, n])).then_inc(cst_dma, 16)
            sp.dma_start(wqkv[:, 0, :], Wqkv[0]).then_inc(w_dma, 16)
            sp.dma_start(wo[:, 0, :, :], Wo[0].rearrange("(k p) n -> p k n", p=P)).then_inc(w_dma, 16)
            sp.dma_start(w1[:, :], W1[0]).then_inc(w1_dma, 16)
            def second_weights(layer):
                sp.dma_start(w2[:, 0:2, :], W2[layer, 0:2 * P, :].rearrange("(i p) n -> p i n", p=P)).then_inc(w2_dma, 16)
                sp.dma_start(w2[0:DFF - 2 * P, 2, :], W2[layer, 2 * P:DFF, :]).then_inc(w2_dma, 16)

            second_weights(0)
            sp.dma_start(b2r[:, :, :], b2.unsqueeze(0).to_broadcast([P, DEPTH, C])).then_inc(cols_dma, 16)
            sp.wait_ge(zero_ready, 1)
            with nc.allow_non_contiguous_dma(reason="a few bias columns"):
                sp.dma_start(cols[:, :, 0], ln_g.rearrange("l p -> p l")).then_inc(cols_dma, 16)
                sp.dma_start(cols[:, :, 1], ln_b.rearrange("l p -> p l")).then_inc(cols_dma, 16)
                for half in range(2):
                    for i, (r, m) in enumerate(BLK):
                        sp.dma_start(cols[0:m, :, 2 + 3 * half + i],
                                     b1[:, DFF * half + r:DFF * half + r + m].rearrange("l p -> p l")
                                     ).then_inc(cols_dma, 16)

            def v_copies(g, s):
                U = UPG * g + s
                sp.wait_ge(qkv_ev, 3 * U + 3)
                settle(sp)
                sp.wait_ge(pv_mm, past(U - 1))
                sp.wait_ge(vw_zero, 1)
                k = s % 2
                src = vs[:, s % 4]
                for h in range(2):
                    for w in range(NW):
                        rows = lambda ap: ap.rearrange("p a d -> p (a d)")
                        if w > 0:
                            sp.dma_start(vw[64 * h:64 * h + 64, k, w, h, :],
                                         rows(src[WIN * (w - 1):WIN * (w + 1), h])).then_inc(vw_dma[k], 16)
                            continue
                        sp.dma_start(vw[64 * h + WIN:64 * h + 64, k, w, h, :],
                                     rows(src[0:WIN, h])).then_inc(vw_dma[k], 16)
                        if s // HALVES > 0:
                            sp.dma_start(vw[64 * h:64 * h + WIN, k, w, h, :],
                                         rows(vs[P - WIN:P, (s - 2) % 4, h])).then_inc(vw_dma[k], 16)

            def next_weights(g):
                q = INNER * 3 // 4
                layer, part = (g // B + 1) % DEPTH, g % B
                place = (g // B + 1) % 2
                sp.dma_start(wqkv[:, place, bass.ds(part * q, q)], Wqkv[layer, :, bass.ds(part * q, q)]).then_inc(w_dma, 16)
                sp.dma_start(wo[:, place, bass.ds(2 * part, 2), :],
                             Wo[layer, bass.ds(2 * P * part, 2 * P), :].rearrange("(k p) n -> p k n", p=P)
                             ).then_inc(w_dma, 16)

            def body(g):
                for s in range(UPG):
                    v_copies(g, s)
                    if s == 4:
                        sp.wait_ge(qkv_mm, past(3 * UPG * g))
                        if has_group(g, 1):
                            sp.wait_ge(turn_mm, turn(g, "y3"))
                        settle(sp)
                        next_weights(g)
                if has_group(g, 1):
                    sp.wait_ge(a_mm, past(3 * g))
                    settle(sp)
                    sp.dma_start(w1[:, :], W1[g // B]).then_inc(w1_dma, 16)
                    sp.wait_ge(turn_mm, turn(g, "down"))
                    settle(sp)
                    second_weights(g // B)

            body(0)
            with sp.Fori(1, GROUPS) as g:
                body(g)
            ot = out.rearrange("b (t p) c -> p (b t) c", p=P)
            for b in range(B):
                sp.wait_ge(fin, b + 1)
                sp.dma_start(ot[:, TPG * b:TPG * (b + 1), :], x1[:, TPG * b:TPG * (b + 1), :]).then_inc(out_dma, 16)
            sp.wait_ge(out_dma, 16 * B)

        @block.tensor
        def _(pe):
            pe.wait_ge(cst_dma, 16 * 9)
            pe.wait_ge(wx_dma, 16 * 5)
            for i in range(4):
                mm = pe.transpose(ps[0][:, i * C:(i + 1) * C], wx_in[:, i, :], ident)
            mm.then_inc(wxT_mm, 1)
            for b in range(B):
                mm = pe.transpose(ps[1][:, b * CTX:(b + 1) * CTX], ctx_sb[:, b, :], ident[0:CTX, 0:CTX])
            mm.then_inc(ctxT_mm, 1)
            pe.wait_ge(wxT_ev, 1)
            pe.wait_ge(ctxT_ev, 1)
            pe.wait_ge(cst_ready, 4)
            pe.matmul(ps[2][:, 0:B * CTX], wxT[:, 1, :], ctxT[:, :, :].rearrange("p b s -> p (b s)"),
                      start=True, stop=True).then_inc(kx_mm, 1)
            pe.wait_ge(small_dma, 16 * 6)
            for b in range(B):
                o_ = ps[3][0:CTX, b * C:(b + 1) * C]
                pe.matmul(o_, ones[0:1, 0:CTX], brow[0:1, 0, :], start=True, stop=False)
                mm = pe.matmul(o_, ctxT[:, b, :], wxT[:, 2, :], start=False, stop=True)
            mm.then_inc(vx_mm, 1)
            pe.wait_ge(kx_ev, 1)
            pe.wait_ge(vx_ev, 1)
            with pe.Fori(0, B) as b:
                pe.wait_ge(a_xn, 4 * b + 4)
                for t in range(TPG):
                    mm = pe.transpose(ps[0][:, t * P:(t + 1) * P], xn[:, t, :], ident)
                mm.then_inc(a_xnT, 1)
                pe.wait_ge(a_xnTev, b + 1)
                pe.matmul(ps[1][:, :], wxT[:, 0, :], xnT[:, :], start=True, stop=True).then_inc(a_q, 1)
                pe.wait_ge(a_qev, b + 1)
                for t in range(TPG):
                    mm = pe.matmul(ps[2][:, t * P:t * P + CTX], xsT[:, t * P:(t + 1) * P], kxT[:, b, :],
                                   start=True, stop=True)
                mm.then_inc(a_sc, 1)
                pe.wait_ge(a_pn, b + 1)
                for t in range(TPG):
                    mm = pe.transpose(ps[3][0:CTX, t * P:(t + 1) * P], xf[:, t, 0:CTX], ident)
                mm.then_inc(a_pT, 1)
                pe.wait_ge(a_pTev, b + 1)
                for t in range(TPG):
                    mm = pe.matmul(ps[4][:, t * P:(t + 1) * P], uT[0:CTX, 0, t * P:(t + 1) * P], vx[:, b, :],
                                   start=True, stop=True)
                mm.then_inc(a_att, 1)
                pe.wait_ge(a_res, b + 1)
                for t in range(TPG):
                    mm = pe.transpose(ps[5][:, t * P:(t + 1) * P], xa[:, t, :], ident)
                mm.then_inc(a_rT, 1)
                pe.wait_ge(a_rTev, b + 1)
                for t in range(TPG):
                    o_ = ps[6][:, t * P:(t + 1) * P]
                    pe.matmul(o_, ones[0:1, :], brow[0:1, 1, :], start=True, stop=False)
                    mm = pe.matmul(o_, uT[:, 1, t * P:(t + 1) * P], wxT[:, 3, :], start=False, stop=True)
                mm.then_inc(a_y, 1)

            def shift(xg, inc):
                pe.matmul(SHARED[:, 0:TPG * 64], down1, xg(0, TPG), start=True, stop=True)
                pe.matmul(SHARED[:, 64:TPG * 64], wrap, xg(0, TPG - 1), start=False, stop=True,
                          skip_group_check=True).then_inc(inc, 1)

            def x_transposes(inc):
                for t in range(TPG):
                    mm = pe.transpose(SHARED[:, t * P:(t + 1) * P], xa[:, t, :], ident)
                mm.then_inc(inc, 1)

            pe.wait_ge(b_x, ahead(B * TPG))
            shift(lambda a, n: x[:, a:a + n, 64:C], p_shift)
            pe.wait_ge(p_up, 1)
            pe.wait_ge(p_low, 1)
            x_transposes(p_xT)

            def take_turn(g, name):
                pe.wait_ge(turn_read, past(turn(g, name) - 1))

            def body(g):
                own, prev = has_group(g, 0), has_group(g, 1)
                for s in range(UPG):
                    U = UPG * g + s
                    t, half = s // HALVES, s % HALVES
                    if own:
                        if s == 0:
                            pe.wait_ge(xsT_ev, g + 1)
                            pe.wait_ge(w_dma, past(16 * 2 * (g + 1)))
                        for i in range(3):
                            n = 3 * U + i
                            pe.wait_ge(qkv_ev, past(n - 1))
                            cols_ = slice(i * INNER + half * UW, i * INNER + half * UW + UW)
                            pe.matmul(QKV_BANKS[(3 * s + i) % 2][:, :], xsT[:, t * P:(t + 1) * P],
                                      wqkv[:, (g // B) % 2, cols_], start=True, stop=True).then_inc(qkv_mm, 1)
                    if s % 2 == 1 and alive(g, s, 4):
                        tile = (s - 4) // 2 % TPG
                        gy = g if s >= 4 else g - 1
                        name = f"y{tile}"
                        take_turn(g, name)
                        pe.wait_ge(oT_ev, past(U - 3))
                        for k in range(INNER // P):
                            mm = pe.matmul(SHARED[:, 0:C], oT[:, tile % 2, k, :], wo[:, (gy // B) % 2, k, :],
                                           start=(k == 0), stop=(k == INNER // P - 1))
                        mm.then_inc(turn_mm, 1)
                    if own and s == 7:
                        take_turn(g, "x_t")
                        pe.wait_ge(xa_low, g + 1)
                        x_transposes(turn_mm)
                    if alive(g, s, 2):
                        pe.wait_ge(exp_done, past(U - 1))
                        pe.wait_ge(oT_ev, past(U - 3))
                        for k in range(HP):
                            mm = pe.transpose(PT_BANK[:, k * P:(k + 1) * P], pr[:, s % 2, k * P:(k + 1) * P], ident)
                        mm.then_inc(pT_mm, 1)
                    if alive(g, s, 1):
                        pe.wait_ge(qkn_done, past(U))
                        pe.wait_ge(qT_ev, past(U - 1))
                        for k in range(HP):
                            mm = pe.transpose(QT_BANK[:, k * P:(k + 1) * P], qkn[:, (s - 1) % 2, k * P:(k + 1) * P], ident)
                        mm.then_inc(qT_mm, 1)
                        pe.wait_ge(kT_ev, past(2 * (U - 1)))
                        if prev and s == 7:
                            pe.wait_ge(u_done, ahead(3 * g))
                        for k in range(HP):
                            mm = pe.transpose(KT_BANK[:, k * P:(k + 1) * P],
                                              qkn[:, (s - 1) % 2, UW + k * P:UW + (k + 1) * P], ident)
                        mm.then_inc(kT_mm, 1)
                    if alive(g, s, 2):
                        gv = g if s >= 2 else g - 1
                        sv = (s - 2) % UPG
                        pe.wait_ge(pT_ev, past(U - 1))
                        pe.wait_ge(vw_dma[sv % 2], vw_count(gv, sv))
                        pe.wait_ge(o_done, past(U - 2))
                        for k in range(HP):
                            for w in range(NW):
                                mm = pe.matmul(heads(PV_BANK[WIN * w:WIN * (w + 1), k * P:(k + 1) * P]),
                                               pT[:, s % 2, k, WIN * w:WIN * (w + 1)],
                                               vw[:, sv % 2, w, :, k * DH:(k + 1) * DH], start=True, stop=True,
                                               tile_position=(0, WIN * w))
                        mm.then_inc(pv_mm, 1)
                    if alive(g, s, 3):
                        pe.wait_ge(o_done, past(U - 2))
                        if alive(g, s, 2):
                            pe.wait_ge(pT_ev, past(U - 1))
                        else:
                            pe.wait_ge(oT_ev, past(U - 3))
                        for k in range(HP):
                            mm = pe.transpose(PT_BANK[:, k * P:(k + 1) * P], o[:, k * P:(k + 1) * P], ident)
                        mm.then_inc(oT_mm, 1)
                    if alive(g, s, 1):
                        sk = (s - 1) % UPG
                        tk, hk = sk // HALVES, sk % HALVES
                        pe.wait_ge(qT_ev, past(U))
                        pe.wait_ge(kT_ev, past(2 * U))
                        pe.wait_ge(sub_done, past(U - 1))
                        pe.matmul(heads(SC_BANK[:, :]), ident_b[:, :],
                                  mask_b[:, min(tk, 1), :].unsqueeze(1).to_broadcast([P, HU, 2 * WIN]),
                                  start=True, stop=True)
                        for k in range(HP):
                            for w in range(NW):
                                c0 = P * tk + WIN * w
                                mm = pe.matmul(heads(SC_BANK[WIN * w:WIN * (w + 1), k * P:(k + 1) * P]),
                                               qT[:, sk % 2, k, WIN * w:WIN * (w + 1)],
                                               kB[:, HP * hk + k, :, c0:c0 + 2 * WIN],
                                               start=False, stop=True, tile_position=(0, WIN * w),
                                               skip_group_check=True)
                        mm.then_inc(score_mm, 1)
                    if own and s == 2:
                        take_turn(g, "shift_att")
                        b = (g + 1) % B
                        shift(lambda a, n: x[:, bass.ds(TPG * b + a, n), 64:C], turn_mm)
                    if prev and s == 4:
                        take_turn(g, "shift_ffn")
                        pe.wait_ge(att_res, past(TPG * g))
                        b = (g + B - 1) % B
                        shift(lambda a, n: x[:, bass.ds(TPG * b + a, n), 64:C], turn_mm)
                    if prev and s == 5:
                        take_turn(g, "ln_t")
                        pe.wait_ge(f_xn, ahead(TPG * g))
                        for t_ in range(TPG):
                            mm = pe.transpose(SHARED[:, t_ * P:(t_ + 1) * P], xn[:, t_, :], ident)
                        mm.then_inc(turn_mm, 1)
                    if prev and s == 6:
                        pe.wait_ge(xnT_done, past(g))
                        pe.wait_ge(w1_dma, past(16 * g))
                        pe.wait_ge(kT_ev, past(2 * U if own else 2 * UNITS))
                        for i, (r, m) in enumerate(BLK):
                            take_turn(g, f"gate{i}")
                            pe.matmul(SHARED[0:m, :], w1[:, DFF + r:DFF + r + m], xnT[:, :],
                                      start=True, stop=True).then_inc(turn_mm, 1)
                            pe.wait_ge(u_done, ahead(3 * g - 3 + i))
                            pe.matmul(KT_BANK[0:m, :], w1[:, r:r + m], xnT[:, :],
                                      start=True, stop=True).then_inc(a_mm, 1)
                    if prev and s == 7:
                        take_turn(g, "down")
                        pe.wait_ge(u_done, ahead(3 * g))
                        pe.wait_ge(w2_dma, past(32 * g))
                        for t_ in range(TPG):
                            for i, (r, m) in enumerate(BLK):
                                mm = pe.matmul(SHARED[:, t_ * P:(t_ + 1) * P], uT[0:m, i, t_ * P:(t_ + 1) * P],
                                               w2[0:m, i, :], start=(i == 0), stop=(i == len(BLK) - 1))
                        mm.then_inc(turn_mm, 1)

            body(0)
            with pe.Fori(1, GROUPS) as g:
                body(g)
            body(GROUPS)

        @block.scalar
        def _(act):
            act.wait_ge(small_dma, 16 * 6)
            act.activation(tg[:, :], gcol[:, :], ACT.Tanh).then_inc(tanh_ready, 1)
            act.wait_ge(wxT_mm, 1)
            act.activation(wxT[:, :, :].rearrange("p a c -> p (a c)"), ps[0][:, :], ACT.Copy).then_inc(wxT_ev, 1)
            act.wait_ge(ctxT_mm, 1)
            act.activation(ctxT[:, :, :].rearrange("p b s -> p (b s)"), ps[1][:, 0:B * CTX], ACT.Copy).then_inc(ctxT_ev, 1)
            act.wait_ge(kx_mm, 1)
            act.activation(kxT[:, :, :].rearrange("p b s -> p (b s)"), ps[2][:, 0:B * CTX], ACT.Identity,
                           bias=bcol[:, 1:2]).then_inc(kx_ev, 1)
            act.wait_ge(vx_mm, 1)
            act.activation(vx[:, :, :].rearrange("p b c -> p (b c)"), ps[3][0:CTX, :], ACT.Copy).then_inc(vx_ev, 1)
            with act.Fori(0, B) as b:
                act.wait_ge(a_xnT, b + 1)
                act.activation(xnT[:, :], ps[0][:, :], ACT.Copy).then_inc(a_xnTev, 1)
                act.wait_ge(a_q, b + 1)
                act.activation(xsT[:, :], ps[1][:, :], ACT.Identity, bias=bcol[:, 0:1]).then_inc(a_qev, 1)
                act.wait_ge(a_sub, b + 1)
                act.activation(xf[:, :, 0:CTX], xf[:, :, 0:CTX], ACT.Exp, scale=float(C) ** -0.5).then_inc(a_exp, 1)
                act.wait_ge(a_pT, b + 1)
                act.activation(uT[0:CTX, 0, :], ps[3][0:CTX, :], ACT.Copy).then_inc(a_pTev, 1)
                act.wait_ge(a_rT, b + 1)
                act.activation(uT[:, 1, :], ps[5][:, :], ACT.Copy).then_inc(a_rTev, 1)
            act.wait_ge(b_x, ahead(B * TPG))
            act.activation(xa[:, :, 0:64], x[:, 0:TPG, 0:64], ACT.Copy).then_inc(p_low, 1)
            act.wait_ge(p_xT, 1)
            act.activation(xsT[:, :], SHARED[:, :], ACT.Copy).then_inc(xsT_ev, 1)
            act.wait_ge(zero_ready, 2)

            def body(g):
                own, prev = has_group(g, 0), has_group(g, 1)
                for s in range(UPG):
                    U = UPG * g + s
                    if own:
                        act.wait_ge(sq_done, past(U - 1))
                        act.wait_ge(cos_done, past(U - 1))
                        act.wait_ge(sin_done, past(U - 1))
                        for i in range(2):
                            act.wait_ge(qkv_mm, 3 * U + i + 1)
                            act.activation(qk[:, s % 2, i * UW:(i + 1) * UW], QKV_BANKS[(3 * s + i) % 2][:, :],
                                           ACT.Copy).then_inc(qkv_ev, 1)
                    if alive(g, s, 2):
                        act.wait_ge(sub_done, past(U - 1))
                        act.wait_ge(pT_mm, past(U - 3))
                        act.wait_ge(sum_done, past(U - 3))
                        act.activation(pr[:, s % 2, :], pr[:, s % 2, :], ACT.Exp).then_inc(exp_done, 1)
                    if own:
                        act.wait_ge(qkv_ev, 3 * U + 2)
                        act.wait_ge(ss_done, past(U))
                        act.activation(sq[:, :], qk[:, s % 2, :], ACT.Square).then_inc(sq_done, 1)
                        act.wait_ge(qkv_mm, 3 * U + 3)
                        if alive(g, s, 2):
                            s2, g2 = (s - 2) % UPG, (g if s >= 2 else g - 1)
                            act.wait_ge(vw_dma[s2 % 2], vw_count(g2, s2))
                        act.activation(vs[:, s % 4], QKV_BANKS[(3 * s + 2) % 2][:, :].rearrange(
                            "p (k h d) -> p h k d", h=2, d=DH), ACT.Copy).then_inc(qkv_ev, 1)
                    if own and s == 7:
                        act.wait_ge(turn_mm, turn(g, "x_t"))
                        act.wait_ge(qkv_mm, 3 * U + 3)
                        act.activation(xsT[:, :], SHARED[:, :], ACT.Copy).then_inc(turn_read, 1)
                        act.wait_ge(turn_read, turn(g, "x_t"))
                        act.sem_inc(xsT_ev, 1)
                    if alive(g, s, 2):
                        act.wait_ge(pT_mm, past(U - 1))
                        act.wait_ge(pv_mm, past(U - 3))
                        act.activation(pT[:, s % 2].rearrange("p k q -> p (k q)"), PT_BANK[:, :],
                                       ACT.Copy).then_inc(pT_ev, 1)
                    if alive(g, s, 1):
                        sk = (s - 1) % UPG
                        tk, hk = sk // HALVES, sk % HALVES
                        act.wait_ge(qT_mm, past(U))
                        act.wait_ge(score_mm, past(U - 2))
                        act.activation(qT[:, sk % 2].rearrange("p k q -> p (k q)"), QT_BANK[:, :],
                                       ACT.Copy).then_inc(qT_ev, 1)
                        act.wait_ge(kT_mm, past(U))
                        act.wait_ge(score_mm, past(U - 6))
                        for h in range(2):
                            act.activation(kB[64 * h:64 * h + 64, HP * hk:HP * hk + HP, h, WIN + P * tk:WIN + P * tk + P],
                                           KT_BANK[64 * h:64 * h + 64, :].rearrange("p (k q) -> p k q", q=P),
                                           ACT.Copy).then_inc(kT_ev, 1)
                    if alive(g, s, 3):
                        so = (s - 3) % UPG
                        to, ho = so // HALVES, so % HALVES
                        act.wait_ge(oT_mm, past(U - 2))
                        if alive(g, s, 3 + 2 * HALVES + ho):
                            act.wait_ge(att_res, past(TPG * g + (s - 3) // HALVES - 1))
                        act.activation(oT[:, to % 2, HP * ho:HP * ho + HP, :].rearrange("p k q -> p (k q)"),
                                       PT_BANK[:, :], ACT.Copy).then_inc(oT_ev, 1)
                    if own and s == 3:
                        act.wait_ge(turn_mm, turn(g, "shift_att"))
                        b = (g + 1) % B
                        src = x[:, bass.ds(TPG * b, TPG), 0:64]
                        act.activation(xa[:, :, 0:64], src, ACT.Copy).then_inc(xa_low, 1)
                    if prev and s == 4:
                        act.wait_ge(att_res, past(TPG * g))
                        b = (g + B - 1) % B
                        src = x[:, bass.ds(TPG * b, TPG), 0:64]
                        act.activation(xf[:, :, 0:64], src, ACT.Copy).then_inc(xf_low, 1)
                    if prev and s == 6:
                        for i, (r, m) in enumerate(BLK):
                            act.wait_ge(turn_mm, turn(g, f"gate{i}"))
                            act.wait_ge(cur_done, past(g))
                            act.activation(uT[0:m, i, :], SHARED[0:m, :], ACT.Gelu,
                                           bias=cur[0:m, 5 + i:6 + i]).then_inc(turn_read, 1)

            body(0)
            with act.Fori(1, GROUPS) as g:
                body(g)
            body(GROUPS)

        @block.vector
        def _(dve):
            for start in (f_xn, f_rstd, u_done, b_x):
                dve.sem_inc(start, 1)
            dve.memset(ones[:, :], 1.0).then_inc(cst_ready, 1)
            dve.memset(minus_half[:, :], -0.5).then_inc(cst_ready, 1)
            dve.wait_ge(cst_dma, 16 * 9)
            dve.tensor_copy(mask_b[:, :, :], mask_f[:, :, :]).then_inc(cst_ready, 1)
            dve.tensor_copy(ident_b[:, :], ident).then_inc(cst_ready, 1)
            dve.wait_ge(tanh_ready, 1)
            dve.wait_ge(x_dma, 32)

            with dve.Fori(0, B) as b:
                def normalise(src, dst, stat, rst, done):
                    settle(dve)
                    for t in range(TPG):
                        dve.bn_stats(stats[:, t, :], src(t)).then_inc(stat, 1)
                    dve.wait_ge(stat, 2 * TPG * b + TPG)
                    settle(dve)
                    for t in range(TPG):
                        dve.bn_aggr(mv[:, t, :], stats[:, t, :]).then_inc(stat, 1)
                    dve.wait_ge(rst, 2 * b + 2)
                    dve.wait_ge(stat, 2 * TPG * b + 2 * TPG)
                    for t in range(TPG):
                        dve.tensor_scalar(dst(t), src(t), mv[:, t, 0:1], rstd[:, t:t + 1], ALU.subtract,
                                          ALU.mult).then_inc(done, 1)

                tile = lambda buf: (lambda t: buf[:, TPG * b + t, :])
                group = bass.ds(TPG * b, TPG)
                dve.wait_ge(b_x, ahead(TPG * b))
                normalise(tile(x1), lambda t: xn[:, t, :], a_stat, a_rstd, a_xn)
                dve.wait_ge(a_sc, b + 1)
                sc = heads(ps[2][:, :], P)[:, :, 0:CTX]
                dve.tensor_reduce(mx4[:, :], sc, AX.X, ALU.max).then_inc(a_mx, 1)
                dve.wait_ge(a_mx, b + 1)
                dve.tensor_tensor(xf[:, :, 0:CTX], sc, spread(mx4[:, :], CTX), ALU.subtract).then_inc(a_sub, 1)
                dve.wait_ge(a_exp, b + 1)
                dve.tensor_reduce(rs4[:, :], xf[:, :, 0:CTX], AX.X, ALU.add).then_inc(a_sum, 1)
                dve.wait_ge(a_sum, b + 1)
                dve.reciprocal(rr4[:, :], rs4[:, :]).then_inc(a_rec, 1)
                dve.wait_ge(a_rec, b + 1)
                dve.tensor_tensor(xf[:, :, 0:CTX], xf[:, :, 0:CTX], spread(rr4[:, :], CTX),
                                  ALU.mult).then_inc(a_pn, 1)
                dve.wait_ge(a_att, b + 1)
                dve.wait_ge(a_xn, 4 * b + 4)
                dve.tensor_tensor(xa[:, :, :], heads(ps[4][:, :], P), xn[:, :, :], ALU.add).then_inc(a_res, 1)
                dve.wait_ge(a_y, b + 1)
                dve.scalar_tensor_tensor(out=x1[:, group, :], in0=heads(ps[6][:, :], P), scalar=tg[:, 0:1],
                                         in1=x1[:, group, :], op0=ALU.mult, op1=ALU.add).then_inc(a_x1, 1)
                dve.wait_ge(a_x1, b + 1)
                normalise(tile(x1), tile(x), b_stat, b_rstd, b_x)
            dve.wait_ge(p_shift, 1)
            dve.tensor_copy(xa[:, :, 64:C], heads(SHARED[:, 0:TPG * 64])).then_inc(p_up, 1)

            def body(g):
                own, prev = has_group(g, 0), has_group(g, 1)
                for s in range(UPG):
                    U = UPG * g + s
                    if alive(g, s, 2):
                        dve.wait_ge(score_mm, past(U - 1))
                        dve.wait_ge(sub_done, past(U - 2))
                        dve.tensor_reduce(mx[:, :], heads(SC_BANK[:, :]), AX.X, ALU.max).then_inc(max_done, 1)
                        dve.wait_ge(max_done, past(U - 1))
                        dve.wait_ge(exp_done, past(U - 3))
                        dve.tensor_tensor(heads(pr[:, s % 2, :]), heads(SC_BANK[:, :]), spread(mx[:, :], DH),
                                          ALU.subtract).then_inc(sub_done, 1)
                    if own:
                        t = s // HALVES
                        if s == 0:
                            dve.wait_ge(table_ready, TPG + g)
                        dve.wait_ge(qkn_done, past(U))
                        dve.wait_ge(qkv_ev, 3 * U + 2)
                        for i in range(2):
                            table = tables[:, (g // B) % 2, t, 2 * DH * i:2 * DH * i + DH]
                            cut = slice(i * UW, (i + 1) * UW)
                            ins = dve.tensor_tensor(heads(ra[:, cut]), heads(qk[:, s % 2, cut]),
                                                    table.unsqueeze(1).to_broadcast([P, HU, DH]), ALU.mult)
                        ins.then_inc(cos_done, 1)
                        dve.wait_ge(sq_done, U + 1)
                        dve.wait_ge(ssm_done, past(U - 1))
                        dve.tensor_reduce(ss[:, s % 2, :], heads(sq[:, :]), AX.X, ALU.add).then_inc(ss_done, 1)
                    if s % 2 == 1 and alive(g, s, 4):
                        tile = (s - 4) // 2 % TPG
                        gy = g if s >= 4 else g + B - 1
                        row = x[:, TPG * (gy % B) + tile, :]
                        dve.wait_ge(turn_mm, turn(g, f"y{tile}"))
                        dve.wait_ge(turn_read, past(turn(g, f"y{tile}") - 1))
                        dve.tensor_tensor(row, row, SHARED[:, 0:C], ALU.add).then_inc(turn_read, 1)
                        dve.wait_ge(turn_read, turn(g, f"y{tile}"))
                        dve.sem_inc(att_res, 1)
                    if alive(g, s, 2):
                        dve.wait_ge(rec_done, past(U - 2))
                        dve.wait_ge(exp_done, past(U - 1))
                        dve.tensor_reduce(rs[:, :], heads(pr[:, s % 2, :]), AX.X, ALU.add).then_inc(sum_done, 1)
                        dve.wait_ge(sum_done, past(U - 1))
                        dve.reciprocal(rr[:, s % 2, :], rs[:, :]).then_inc(rec_done, 1)
                    if own:
                        dve.wait_ge(sin_done, U + 1)
                        dve.wait_ge(cos_done, U + 1)
                        dve.tensor_tensor(ra[:, :], ra[:, :], rb[:, :], ALU.add).then_inc(rot_done, 1)
                    if alive(g, s, 2):
                        dve.wait_ge(rec_done, past(U - 1))
                        dve.wait_ge(pv_mm, past(U - 1))
                        dve.wait_ge(oT_mm, past(U - 2))
                        dve.tensor_tensor(heads(o[:, :]), heads(PV_BANK[:, :]), spread(rr[:, s % 2, :], DH),
                                          ALU.mult).then_inc(o_done, 1)
                    if own:
                        dve.wait_ge(rn_done, U + 1)
                        dve.wait_ge(rot_done, U + 1)
                        dve.wait_ge(kT_mm, past(U - 1))
                        dve.tensor_tensor(heads(qkn[:, s % 2, :]), heads(ra[:, :]), spread(rn[:, s % 2, :], DH),
                                          ALU.mult).then_inc(qkn_done, 1)
                    if own and s == 2:
                        dve.wait_ge(turn_mm, turn(g, "shift_att"))
                        dve.tensor_copy(xa[:, :, 64:C], heads(SHARED[:, 0:TPG * 64])).then_inc(turn_read, 1)
                    if prev and s == 4:
                        dve.wait_ge(f_xn, ahead(TPG * (g - 1)))
                        dve.wait_ge(turn_mm, turn(g, "shift_ffn"))
                        dve.tensor_copy(xf[:, :, 64:C], heads(SHARED[:, 0:TPG * 64])).then_inc(turn_read, 1)
                        dve.wait_ge(turn_read, turn(g, "shift_ffn"))
                        dve.wait_ge(xf_low, past(g))
                        settle(dve)
                        for t_ in range(TPG):
                            dve.bn_stats(stats[:, t_, :], xf[:, t_, :]).then_inc(f_stat, 1)
                        dve.wait_ge(f_stat, past(TPG * g))
                        settle(dve)
                        for t_ in range(TPG):
                            dve.bn_aggr(mv[:, t_, :], stats[:, t_, :]).then_inc(f_aggr, 1)
                        dve.wait_ge(f_aggr, past(TPG * g))
                        dve.wait_ge(f_rstd, ahead(g))
                        for t_ in range(TPG):
                            dve.tensor_scalar(xn[:, t_, :], xf[:, t_, :], mv[:, t_, 0:1], rstd[:, t_:t_ + 1],
                                              ALU.subtract, ALU.mult).then_inc(f_xn, 1)
                    if prev and s == 5:
                        dve.wait_ge(turn_mm, turn(g, "ln_t"))
                        dve.wait_ge(cur_done, past(g))
                        dve.tensor_scalar(xnT[:, :], SHARED[:, :], cur[:, 0:1], cur[:, 1:2], ALU.mult,
                                          ALU.add).then_inc(turn_read, 1)
                        dve.wait_ge(turn_read, turn(g, "ln_t"))
                        dve.sem_inc(xnT_done, 1)
                    if prev and s == 6:
                        for i, (r, m) in enumerate(BLK):
                            dve.wait_ge(a_mm, past(3 * g - 3 + i + 1))
                            dve.wait_ge(turn_read, turn(g, f"gate{i}"))
                            dve.scalar_tensor_tensor(out=uT[0:m, i, :], in0=KT_BANK[0:m, :], scalar=cur[0:m, 2 + i:3 + i],
                                                     in1=uT[0:m, i, :], op0=ALU.add, op1=ALU.mult
                                                     ).then_inc(u_done, 1)
                    if prev and s == 7:
                        b = (g + B - 1) % B
                        rows = x[:, bass.ds(TPG * b, TPG), :]
                        dve.wait_ge(turn_mm, turn(g, "down"))
                        dve.wait_ge(b2_done, past(g))
                        dve.tensor_tensor(rows, rows, heads(SHARED[:, :], C), ALU.add).then_inc(turn_read, 1)

            body(0)
            with dve.Fori(1, GROUPS) as g:
                body(g)
            body(GROUPS)
            dve.wait_ge(turn_read, turn(GROUPS, "down"))
            for b in range(B):
                rows = lambda buf: buf[:, TPG * b:TPG * (b + 1), :].rearrange("p t c -> p (t c)")
                dve.scalar_tensor_tensor(out=rows(x1), in0=rows(x), scalar=tg[:, 1:2], in1=rows(x1),
                                         op0=ALU.mult, op1=ALU.add).then_inc(fin, 1)

        @block.gpsimd
        def _(pool):
            pool.memset(cols[:, :, :], 0.0).then_inc(zero_ready, 1)
            pool.memset(kB[:, :, :, :], 0.0).then_inc(zero_ready, 1)
            pool.wait_ge(cst_ready, 2)

            def inverse_root(b, stat, rst):
                pool.wait_ge(stat, 2 * TPG * b + 2 * TPG)
                settle(pool)
                pool.tensor_scalar(vare[:, :], mv[:, :, 1], LN_EPS, None, ALU.add).then_inc(rst, 1)
                pool.wait_ge(rst, 2 * b + 1)
                pool.tensor_tensor(rstd[:, :], vare[:, :], minus_half[:, 0:TPG], ALU.pow).then_inc(rst, 1)

            with pool.Fori(0, B) as b:
                inverse_root(b, a_stat, a_rstd)
                inverse_root(b, b_stat, b_rstd)

            pool.wait_ge(b_x, ahead(B * TPG))
            pool.memset(free, 0.0).then_inc(vw_zero, 1)
            pool.wait_ge(cst_dma, 16 * 9)
            for t in range(TPG):
                pool.tensor_tensor(tables[:, 0, t, :], rope[:, t, :], scales[:, 0, :], ALU.mult).then_inc(table_ready, 1)

            def body(g):
                own, prev = has_group(g, 0), has_group(g, 1)
                for s in range(UPG):
                    U = UPG * g + s
                    if own:
                        t = s // HALVES
                        if s == 0:
                            pool.wait_ge(table_ready, TPG + g)
                        pool.wait_ge(qkv_ev, 3 * U + 2)
                        pool.wait_ge(rot_done, past(U))
                        settle(pool)
                        for i in range(2):
                            table = tables[:, (g // B) % 2, t, 2 * DH * i + DH:2 * DH * (i + 1)]
                            cut = slice(i * UW, (i + 1) * UW)
                            halves = lambda ap: ap.rearrange("p (h a d) -> p h a d", a=2, d=DH // 2)
                            ins = pool.tensor_tensor(
                                halves(rb[:, cut]), halves(qk[:, s % 2, cut])[:, :, ::-1, :],
                                table.rearrange("p (a d) -> p a d", a=2).unsqueeze(1).to_broadcast([P, HU, 2, DH // 2]),
                                ALU.mult)
                        ins.then_inc(sin_done, 1)
                        pool.wait_ge(rn_done, past(U))
                        pool.wait_ge(ss_done, U + 1)
                        settle(pool)
                        pool.tensor_scalar(ssm[:, :], ss[:, s % 2, :], 1e-24, None, ALU.max).then_inc(ssm_done, 1)
                        pool.wait_ge(ssm_done, U + 1)
                        pool.wait_ge(qkn_done, past(U - 1))
                        pool.tensor_tensor(rn[:, s % 2, :], ssm[:, :], minus_half[:, :], ALU.pow).then_inc(rn_done, 1)
                    if prev and s == 4:
                        pool.wait_ge(f_rstd, ahead(g - 1))
                        pool.wait_ge(f_aggr, past(TPG * g))
                        settle(pool)
                        pool.tensor_scalar(vare[:, :], mv[:, :, 1], LN_EPS, None, ALU.add).then_inc(f_var, 1)
                        pool.wait_ge(f_var, past(g))
                        pool.tensor_tensor(rstd[:, :], vare[:, :], minus_half[:, 0:TPG], ALU.pow).then_inc(f_rstd, 1)
                        if isinstance(g, int):
                            pool.wait_ge(cols_dma, 16 * 9)
                        pool.wait_ge(u_done, ahead(3 * (g - 1)))
                        pool.tensor_copy(cur[:, :], cols[:, (g - 1) // B, :]).then_inc(cur_done, 1)
                        pool.wait_ge(turn_mm, turn(g, "shift_ffn"))
                        pool.wait_ge(xf_low, past(g))
                        settle(pool)
                        b = (g + B - 1) % B
                        rows = x[:, bass.ds(TPG * b, TPG), :]
                        pool.tensor_tensor(rows, rows, b2r[:, (g - 1) // B, :].unsqueeze(1).to_broadcast([P, TPG, C]),
                                           ALU.add).then_inc(b2_done, 1)
                    if own and s == 7:
                        layer, place, part = (g // B + 1) % DEPTH, (g // B + 1) % 2, g % B
                        pool.wait_ge(cos_done, past(UPG * g))
                        settle(pool)
                        pool.tensor_tensor(tables[:, place, part, :], rope[:, part, :], scales[:, layer, :],
                                           ALU.mult).then_inc(table_ready, 1)

            pool.wait_ge(cols_dma, 16 * 9)
            body(0)
            with pool.Fori(1, GROUPS) as g:
                body(g)
            body(GROUPS)


_INS = ["x", "ctx_1024", "g_xattn", "g_ffn", "L0_xattn_Wq", "L0_xattn_bq", "L0_xattn_Wk", "L0_xattn_bk", "L0_xattn_Wv",
        "L0_xattn_bv", "L0_xattn_Wo", "L0_xattn_bo", "L0_ffn_Wqkv", "L0_ffn_q_scale", "L0_ffn_k_scale", "L0_ffn_Wo",
        "L0_ffn_ln_g", "L0_ffn_ln_b", "L0_ffn_W1", "L0_ffn_b1", "L0_ffn_W2", "L0_ffn_b2"]


def kernel(**inputs):
    import numpy as _np
    import concourse.bacc as _bacc
    from concourse import mybir as _mybir
    from concourse.bass_utils import run_bass_kernel_spmd as _run

    nc = _bacc.Bacc("TRN2", target_bir_lowering=False, num_devices=1)
    arrays, args = {}, []
    given = [(n, _np.ascontiguousarray(inputs[n])) for n in _INS]
    given += list(zip(("rope", "mats", "mask"), constants()))
    for name, a in given:
        arrays[f"in_{name}_dram"] = a
        args.append(nc.dram_tensor(f"in_{name}_dram", a.shape, _mybir.dt.from_np(a.dtype), kind="ExternalInput").ap())
    out = nc.dram_tensor("out_0_dram", (B, N, C), _mybir.dt.float32, kind="ExternalOutput").ap()
    build(nc, *args, out)
    r = _run(nc, [arrays], core_ids=[0])
    return r.results[0]["out_0_dram"]
```

```python
from contextlib import ExitStack

import numpy as np

import concourse.bass as bass
from concourse import mybir

F32 = mybir.dt.float32
BF16 = mybir.dt.bfloat16
ALU = mybir.AluOpType
ACT = mybir.ActivationFunctionType
AX = mybir.AxisListType

P = 128
B, N, C = 4, 512, 128
CTX = 77
DEPTH, HEADS, DH, WIN = 6, 16, 64, 32
INNER = HEADS * DH
DFF = 341
TPG = N // P
GROUPS = DEPTH * B
HALVES = 2
UPG = TPG * HALVES
UNITS = GROUPS * UPG
HU = HEADS // HALVES
HP = HU // 2
UW = HU * DH
NW = P // WIN
BLK = [(0, 128), (128, 128), (256, DFF - 256)]
LN_EPS = 1e-5
NORM_MIN = 1e-12
LN_SHIFT = 2.0 ** 16

TURNS = ["y2", "shift_att", "y3", "shift_ffn", "y0", "ln_t", "gate0", "a1", "y1", "x_t"]
FIRST_TURNS = ["shift_att", "y0", "y1", "x_t"]
LAST_TURNS = ["y2", "y3", "shift_ffn", "ln_t", "gate0", "a1"]


def turn(g, name):
    if isinstance(g, int) and g == 0:
        return FIRST_TURNS.index(name) + 1
    lacking = len(TURNS) - len(FIRST_TURNS)
    order = LAST_TURNS if isinstance(g, int) and g == GROUPS else TURNS
    return len(TURNS) * g - lacking + order.index(name) + 1


def constants():
    f = np.float32
    half = np.arange(0, DH, 2, dtype=f)
    inv_freq = (f(1.0) / f(10000.0) ** (half / f(DH))).astype(f)
    t = np.arange(N, dtype=f)
    freqs = t[:, None] * inv_freq[None, :]
    base = (half + f(0.4 * DH)) / f(1.4 * DH)
    power = (t - f(N // 2)) / f(WIN // 2)
    scale = base[None, :] ** power[:, None]
    inv = f(1.0) / scale
    cos, sin = np.cos(freqs), np.sin(freqs)
    both = lambda a, b: np.concatenate([a, b], 1)
    qk_scale = f(8.0)
    tables = np.concatenate([
        both(cos * scale, cos * scale) * qk_scale, both(-sin * scale, sin * scale) * qk_scale,
        both(cos * inv, cos * inv), both(-sin * inv, sin * inv)], 1).astype(f)
    rope = tables.reshape(TPG, P, 4 * DH).transpose(1, 0, 2)
    ident = np.eye(P, dtype=f)
    down1 = np.eye(P, k=1, dtype=f)
    wrap = np.zeros((P, P), f)
    wrap[P - 1, 0] = 1.0
    i = np.arange(P)[:, None] % WIN
    j = np.arange(2 * WIN)[None, :]
    seen = (j >= i) & (j <= i + WIN)
    first = seen & ((np.arange(P)[:, None] >= WIN) | (j >= WIN))
    mask = np.where(np.stack([first, seen], 1), f(0.0), f(-3.0e38)).astype(f)
    return (np.ascontiguousarray(rope), np.concatenate([ident, down1, wrap], 1),
            np.ascontiguousarray(mask))


def build(nc, x_in, ctx_in, g_xattn, g_ffn, Wq, bq, Wk, bk, Wv, bv, Wo_x, bo, Wqkv, q_scale, k_scale,
          Wo, ln_g, ln_b, W1, b1, W2, b2, rope_in, mats_in, mask_in, out):
    ctx = ExitStack()
    with ctx:
        def sb(name, shape, dt=F32):
            return ctx.enter_context(nc.sbuf_tensor(name, shape, dt))

        def sem(name):
            return ctx.enter_context(nc.semaphore(name))

        ps = [ctx.enter_context(nc.psum_tensor(f"bank{i}", [P, 512], F32)) for i in range(8)]
        QKV_BANKS, QT_BANK, KT_BANK, SC_BANK, PT_BANK, PV_BANK, SHARED = ps[0:2], ps[2], ps[3], ps[4], ps[5], ps[6], ps[7]

        mats = sb("mats", [P, 3 * P])
        ident, down1, wrap = mats[:, 0:P], mats[:, P:2 * P], mats[:, 2 * P:3 * P]
        mask_f = sb("mask_f", [P, 2, 2 * WIN])
        mask_b = sb("mask_b", [P, 2, 2 * WIN], BF16)
        ident_b = sb("ident_b", [P, P], BF16)
        rope = sb("rope", [P, TPG, 4 * DH])
        scales = sb("scales", [P, DEPTH, 4 * DH])
        tables = sb("tables", [P, 2, TPG, 4 * DH])
        wqkv = sb("wqkv", [P, 2, 3 * INNER])
        wo = sb("wo", [P, 2, INNER // P, C])
        w1 = sb("w1", [P, DFF + len(BLK) * P])
        w2 = sb("w2", [P, len(BLK), C])
        b2r = sb("b2r", [P, DEPTH, C])
        cols = sb("cols", [P, DEPTH, 8])
        cur = sb("cur", [P, 8])
        x1 = sb("x1", [P, B * TPG, C])
        x = sb("x", [P, B * TPG, C])
        xa = sb("xa", [P, TPG, C])
        xsT = sb("xsT", [P, N])
        xf = sb("xf", [P, TPG, C])
        xn = sb("xn", [P, TPG, C])
        xnT = sb("xnT", [P, N])
        uT = sb("uT", [P, len(BLK), N])
        stats = sb("stats", [P, TPG, 6])
        mv = sb("mv", [P, TPG, 2])
        vare = sb("vare", [P, TPG])
        rstd = sb("rstd", [P, TPG])
        f_tmp = sb("f_tmp", [P, TPG])
        f_seed = sb("f_seed", [P, TPG])
        minus_half = sb("minus_half", [P, 2 * HU])
        qk = sb("qk", [P, 2, 2 * UW])
        sq = sb("sq", [P, 2 * UW])
        ra = sb("ra", [P, 2 * UW])
        rb = sb("rb", [P, 2 * UW])
        qkn = sb("qkn", [P, 2, 2 * UW])
        ss = sb("ss", [P, 2 * HU])
        ssm = sb("ssm", [P, 2 * HU])
        lnn = sb("lnn", [P, 2 * HU])
        seed = sb("seed", [P, 2 * HU])
        step = sb("step", [P, 2 * HU])
        rn = sb("rn", [P, 2 * HU])
        shift_back = sb("shift_back", [P, 1])
        qT = sb("qT", [P, 2, HP, P])
        kB = sb("kB", [P, HALVES * HP, 2, WIN + N])
        vs = sb("vs", [P, 4, 2, HP, DH])
        vw = sb("vw", [P, 2, NW, 2, HP * DH])
        pr = sb("pr", [P, 2, UW])
        pT = sb("pT", [P, 2, HP, P])
        o = sb("o", [P, UW])
        oT = sb("oT", [P, 2, INNER // P, P])
        mx = sb("mx", [P, HU])
        rs = sb("rs", [P, HU])
        rr = sb("rr", [P, 2, HU])
        free = vw[:, :, :, :, :].rearrange("p k w h n -> p (k w h n)")

        def take(start, groups, width):
            return free[:, start:start + groups * width].rearrange("p (a c) -> p a c", c=width)

        wx_in, wxT = take(0, 4, C), take(512, 4, C)
        ctx_sb, vx = take(1024, B, C)[0:CTX], take(1536, B, C)[0:CTX]
        ctxT, kxT = take(2048, B, CTX), take(2560, B, CTX)
        bcol = sb("bcol", [P, 2])
        brow = sb("brow", [1, 2, C])
        ones = sb("ones", [1, P])
        gcol = sb("gcol", [P, 2])
        tg = sb("tg", [P, 2])
        mx4 = sb("mx4", [P, TPG])
        rs4 = sb("rs4", [P, TPG])
        rr4 = sb("rr4", [P, TPG])

        x_dma = sem("x_dma")
        cst_dma = sem("cst_dma")
        small_dma = sem("small_dma")
        wx_dma = sem("wx_dma")
        w_dma = sem("w_dma")
        w1_dma = sem("w1_dma")
        w2_dma = sem("w2_dma")
        cols_dma = sem("cols_dma")
        out_dma = sem("out_dma")
        cst_ready = sem("cst_ready")
        settled = sem("settled")
        zero_ready = sem("zero_ready")
        w1_pad = sem("w1_pad")
        vw_zero = sem("vw_zero")
        tanh_ready = sem("tanh_ready")
        table_ready = sem("table_ready")
        wxT_mm = sem("wxT_mm")
        wxT_ev = sem("wxT_ev")
        ctxT_mm = sem("ctxT_mm")
        ctxT_ev = sem("ctxT_ev")
        kx_mm = sem("kx_mm")
        kx_ev = sem("kx_ev")
        vx_mm = sem("vx_mm")
        vx_ev = sem("vx_ev")
        a_stat = sem("a_stat")
        a_rstd = sem("a_rstd")
        a_xn = sem("a_xn")
        a_xnT = sem("a_xnT")
        a_xnTev = sem("a_xnTev")
        a_q = sem("a_q")
        a_qev = sem("a_qev")
        a_sc = sem("a_sc")
        a_mx = sem("a_mx")
        a_sub = sem("a_sub")
        a_exp = sem("a_exp")
        a_sum = sem("a_sum")
        a_rec = sem("a_rec")
        a_pn = sem("a_pn")
        a_pT = sem("a_pT")
        a_pTev = sem("a_pTev")
        a_att = sem("a_att")
        a_res = sem("a_res")
        a_rT = sem("a_rT")
        a_rTev = sem("a_rTev")
        a_y = sem("a_y")
        a_x1 = sem("a_x1")
        b_stat = sem("b_stat")
        b_rstd = sem("b_rstd")
        b_x = sem("b_x")
        p_shift = sem("p_shift")
        p_up = sem("p_up")
        p_low = sem("p_low")
        p_xT = sem("p_xT")
        qkv_mm = sem("qkv_mm")
        qkv_ev = sem("qkv_ev")
        sq_done = sem("sq_done")
        cos_done = sem("cos_done")
        sin_done = sem("sin_done")
        ss_done = sem("ss_done")
        ssm_done = sem("ssm_done")
        ln_done = sem("ln_done")
        seed_done = sem("seed_done")
        newton_done = sem("newton_done")
        rn_done = sem("rn_done")
        rotq_done = sem("rotq_done")
        rotk_done = sem("rotk_done")
        qn_done = sem("qn_done")
        kn_done = sem("kn_done")
        qT_mm = sem("qT_mm")
        kT_mm = sem("kT_mm")
        qT_ev = sem("qT_ev")
        kT_ev = sem("kT_ev")
        score_mm = sem("score_mm")
        max_done = sem("max_done")
        sub_done = sem("sub_done")
        exp_done = sem("exp_done")
        sum_done = sem("sum_done")
        rec_done = sem("rec_done")
        pT_mm = sem("pT_mm")
        pT_ev = sem("pT_ev")
        pv_mm = sem("pv_mm")
        o_done = sem("o_done")
        oT_mm = sem("oT_mm")
        oT_ev = sem("oT_ev")
        att_res = sem("att_res")
        turn_mm = sem("turn_mm")
        turn_read = sem("turn_read")
        xa_low = sem("xa_low")
        xsT_ev = sem("xsT_ev")
        xf_low = sem("xf_low")
        f_stat = sem("f_stat")
        f_aggr = sem("f_aggr")
        f_var = sem("f_var")
        f_rstd = sem("f_rstd")
        f_xn = sem("f_xn")
        b2_done = sem("b2_done")
        cur_done = sem("cur_done")
        xnT_done = sem("xnT_done")
        f_ln = sem("f_ln")
        f_seeded = sem("f_seeded")
        f_newton = sem("f_newton")
        gate_mm = sem("gate_mm")
        gate_read = sem("gate_read")
        a_mm = sem("a_mm")
        down_mm = sem("down_mm")
        down_read = sem("down_read")
        u_done = sem("u_done")
        fin = sem("fin")
        vw_dma = [sem(f"vw_dma{i}") for i in range(2)]

        def past(count):
            return max(count, 0) if isinstance(count, int) else count

        def ahead(count):
            return count + 1

        def settle(eng):
            eng.sem_inc(settled, 1)

        def alive(g, s, lag):
            if isinstance(g, int) and g == 0:
                return s >= lag
            if isinstance(g, int) and g == GROUPS:
                return s < lag
            return True

        def has_group(g, back):
            if isinstance(g, int) and g == 0:
                return back == 0
            if isinstance(g, int) and g == GROUPS:
                return back == 1
            return True

        def heads(ap, d=DH):
            return ap.rearrange("p (h d) -> p h d", d=d)

        def spread(ap, n):
            return ap.unsqueeze(2).to_broadcast([P, ap.shape[1], n])

        def vw_count(g, s):
            per_unit = 2 * (NW + 1)
            per_group = per_unit * TPG - 2
            return 16 * (per_group * g + per_unit * (s // HALVES + 1) - 2)

        block = ctx.enter_context(nc.Block())

        @block.sync
        def _(sp):
            xt = x_in.rearrange("b (t p) c -> p (b t) c", p=P)
            sp.dma_start(x1[:, 0:TPG, :], xt[:, 0:TPG, :]).then_inc(x_dma, 16)
            sp.dma_start(mats[:, :], mats_in).then_inc(cst_dma, 16)
            sp.dma_start(mask_f[:, :, :], mask_in).then_inc(cst_dma, 16)
            sp.dma_start(ctx_sb[:, :, :], ctx_in.rearrange("b s c -> s b c")).then_inc(wx_dma, 16)
            for i, w in enumerate((Wq, Wk, Wv, Wo_x)):
                sp.dma_start(wx_in[:, i, :], w).then_inc(wx_dma, 16)
            sp.dma_start(bcol[:, 0:1], bq.unsqueeze(1)).then_inc(small_dma, 16)
            sp.dma_start(bcol[:, 1:2], bk.unsqueeze(1)).then_inc(small_dma, 16)
            sp.dma_start(brow[:, 0, :], bv.unsqueeze(0)).then_inc(small_dma, 16)
            sp.dma_start(brow[:, 1, :], bo.unsqueeze(0)).then_inc(small_dma, 16)
            sp.dma_start(gcol[:, 0:1], g_xattn.unsqueeze(0).to_broadcast([P, 1])).then_inc(small_dma, 16)
            sp.dma_start(gcol[:, 1:2], g_ffn.unsqueeze(0).to_broadcast([P, 1])).then_inc(small_dma, 16)
            sp.dma_start(x1[:, TPG:, :], xt[:, TPG:, :]).then_inc(x_dma, 16)
            sp.dma_start(rope[:, :, :], rope_in).then_inc(cst_dma, 16)
            h = DH // 2
            for i, s in enumerate((q_scale, k_scale)):
                for dst, src in ((0, 0), (DH, h), (DH + h, 0)):
                    n = DH if dst == 0 else h
                    sp.dma_start(scales[:, :, 2 * DH * i + dst:2 * DH * i + dst + n],
                                 s[:, src:src + n].unsqueeze(0).to_broadcast([P, DEPTH, n])).then_inc(cst_dma, 16)
            sp.dma_start(wqkv[:, 0, :], Wqkv[0]).then_inc(w_dma, 16)
            sp.dma_start(wo[:, 0, :, :], Wo[0].rearrange("(k p) n -> p k n", p=P)).then_inc(w_dma, 16)
            sp.dma_start(w1[:, 0:2 * DFF], W1[0]).then_inc(w1_dma, 16)
            def second_weights(layer):
                sp.dma_start(w2[:, 0:2, :], W2[layer, 0:2 * P, :].rearrange("(i p) n -> p i n", p=P)).then_inc(w2_dma, 16)
                sp.dma_start(w2[0:DFF - 2 * P, 2, :], W2[layer, 2 * P:DFF, :]).then_inc(w2_dma, 16)

            second_weights(0)
            sp.dma_start(b2r[:, :, :], b2.unsqueeze(0).to_broadcast([P, DEPTH, C])).then_inc(cols_dma, 16)
            sp.wait_ge(zero_ready, 1)
            with nc.allow_non_contiguous_dma(reason="a few bias columns"):
                sp.dma_start(cols[:, :, 0], ln_g.rearrange("l p -> p l")).then_inc(cols_dma, 16)
                sp.dma_start(cols[:, :, 1], ln_b.rearrange("l p -> p l")).then_inc(cols_dma, 16)
                for half in range(2):
                    for i, (r, m) in enumerate(BLK):
                        sp.dma_start(cols[0:m, :, 2 + 3 * half + i],
                                     b1[:, DFF * half + r:DFF * half + r + m].rearrange("l p -> p l")
                                     ).then_inc(cols_dma, 16)

            def v_copies(g, s):
                U = UPG * g + s
                sp.wait_ge(qkv_ev, 3 * U + 3)
                settle(sp)
                sp.wait_ge(pv_mm, past(U - 1))
                sp.wait_ge(vw_zero, 1)
                k = s % 2
                src = vs[:, s % 4]
                for h in range(2):
                    for w in range(NW):
                        rows = lambda ap: ap.rearrange("p a d -> p (a d)")
                        if w > 0:
                            sp.dma_start(vw[64 * h:64 * h + 64, k, w, h, :],
                                         rows(src[WIN * (w - 1):WIN * (w + 1), h])).then_inc(vw_dma[k], 16)
                            continue
                        sp.dma_start(vw[64 * h + WIN:64 * h + 64, k, w, h, :],
                                     rows(src[0:WIN, h])).then_inc(vw_dma[k], 16)
                        if s // HALVES > 0:
                            sp.dma_start(vw[64 * h:64 * h + WIN, k, w, h, :],
                                         rows(vs[P - WIN:P, (s - 2) % 4, h])).then_inc(vw_dma[k], 16)

            def next_weights(g):
                q = INNER * 3 // 4
                layer, part = (g // B + 1) % DEPTH, g % B
                place = (g // B + 1) % 2
                sp.dma_start(wqkv[:, place, bass.ds(part * q, q)], Wqkv[layer, :, bass.ds(part * q, q)]).then_inc(w_dma, 16)
                sp.dma_start(wo[:, place, bass.ds(2 * part, 2), :],
                             Wo[layer, bass.ds(2 * P * part, 2 * P), :].rearrange("(k p) n -> p k n", p=P)
                             ).then_inc(w_dma, 16)

            def body(g):
                for s in range(UPG):
                    v_copies(g, s)
                    if s == 4:
                        sp.wait_ge(qkv_mm, past(3 * UPG * g))
                        if has_group(g, 1):
                            sp.wait_ge(turn_mm, turn(g, "y3"))
                        settle(sp)
                        next_weights(g)
                if has_group(g, 1):
                    sp.wait_ge(a_mm, past(2 * g))
                    settle(sp)
                    sp.dma_start(w1[:, 0:2 * DFF], W1[g // B]).then_inc(w1_dma, 16)
                    sp.wait_ge(down_mm, past(g))
                    settle(sp)
                    second_weights(g // B)

            body(0)
            with sp.Fori(1, GROUPS) as g:
                body(g)
            ot = out.rearrange("b (t p) c -> p (b t) c", p=P)
            for b in range(B):
                sp.wait_ge(fin, b + 1)
                sp.dma_start(ot[:, TPG * b:TPG * (b + 1), :], x1[:, TPG * b:TPG * (b + 1), :]).then_inc(out_dma, 16)
            sp.wait_ge(out_dma, 16 * B)

        @block.tensor
        def _(pe):
            pe.wait_ge(cst_dma, 16 * 9)
            pe.wait_ge(wx_dma, 16 * 5)
            for i in range(4):
                mm = pe.transpose(ps[0][:, i * C:(i + 1) * C], wx_in[:, i, :], ident)
            mm.then_inc(wxT_mm, 1)
            for b in range(B):
                mm = pe.transpose(ps[1][:, b * CTX:(b + 1) * CTX], ctx_sb[:, b, :], ident[0:CTX, 0:CTX])
            mm.then_inc(ctxT_mm, 1)
            pe.wait_ge(wxT_ev, 1)
            pe.wait_ge(ctxT_ev, 1)
            pe.wait_ge(cst_ready, 5)
            pe.matmul(ps[2][:, 0:B * CTX], wxT[:, 1, :], ctxT[:, :, :].rearrange("p b s -> p (b s)"),
                      start=True, stop=True).then_inc(kx_mm, 1)
            pe.wait_ge(small_dma, 16 * 6)
            for b in range(B):
                o_ = ps[3][0:CTX, b * C:(b + 1) * C]
                pe.matmul(o_, ones[0:1, 0:CTX], brow[0:1, 0, :], start=True, stop=False)
                mm = pe.matmul(o_, ctxT[:, b, :], wxT[:, 2, :], start=False, stop=True)
            mm.then_inc(vx_mm, 1)
            pe.wait_ge(kx_ev, 1)
            pe.wait_ge(vx_ev, 1)
            with pe.Fori(0, B) as b:
                pe.wait_ge(a_xn, 4 * b + 4)
                for t in range(TPG):
                    mm = pe.transpose(ps[0][:, t * P:(t + 1) * P], xn[:, t, :], ident)
                mm.then_inc(a_xnT, 1)
                pe.wait_ge(a_xnTev, b + 1)
                pe.matmul(ps[1][:, :], wxT[:, 0, :], xnT[:, :], start=True, stop=True).then_inc(a_q, 1)
                pe.wait_ge(a_qev, b + 1)
                for t in range(TPG):
                    mm = pe.matmul(ps[2][:, t * P:t * P + CTX], xsT[:, t * P:(t + 1) * P], kxT[:, b, :],
                                   start=True, stop=True)
                mm.then_inc(a_sc, 1)
                pe.wait_ge(a_pn, b + 1)
                for t in range(TPG):
                    mm = pe.transpose(ps[3][0:CTX, t * P:(t + 1) * P], xf[:, t, 0:CTX], ident)
                mm.then_inc(a_pT, 1)
                pe.wait_ge(a_pTev, b + 1)
                for t in range(TPG):
                    mm = pe.matmul(ps[4][:, t * P:(t + 1) * P], uT[0:CTX, 0, t * P:(t + 1) * P], vx[:, b, :],
                                   start=True, stop=True)
                mm.then_inc(a_att, 1)
                pe.wait_ge(a_res, b + 1)
                for t in range(TPG):
                    mm = pe.transpose(ps[5][:, t * P:(t + 1) * P], xa[:, t, :], ident)
                mm.then_inc(a_rT, 1)
                pe.wait_ge(a_rTev, b + 1)
                for t in range(TPG):
                    o_ = ps[6][:, t * P:(t + 1) * P]
                    pe.matmul(o_, ones[0:1, :], brow[0:1, 1, :], start=True, stop=False)
                    mm = pe.matmul(o_, uT[:, 1, t * P:(t + 1) * P], wxT[:, 3, :], start=False, stop=True)
                mm.then_inc(a_y, 1)

            def shift(xg, inc):
                pe.matmul(SHARED[:, 0:TPG * 64], down1, xg(0, TPG), start=True, stop=True)
                pe.matmul(SHARED[:, 64:TPG * 64], wrap, xg(0, TPG - 1), start=False, stop=True,
                          skip_group_check=True).then_inc(inc, 1)

            def x_transposes(inc):
                for t in range(TPG):
                    mm = pe.transpose(SHARED[:, t * P:(t + 1) * P], xa[:, t, :], ident)
                mm.then_inc(inc, 1)

            pe.wait_ge(b_x, ahead(B * TPG))
            shift(lambda a, n: x[:, a:a + n, 64:C], p_shift)
            pe.wait_ge(p_up, 1)
            pe.wait_ge(p_low, 1)
            x_transposes(p_xT)

            def project(g, s, i):
                n, t, half = 3 * (UPG * g + s) + i, s // HALVES, s % HALVES
                pe.wait_ge(qkv_ev, past(n - 1))
                cut = slice(i * INNER + half * UW, i * INNER + half * UW + UW)
                pe.matmul(QKV_BANKS[(3 * s + i) % 2][:, :],
                          xsT[:, t * P:(t + 1) * P], wqkv[:, (g // B) % 2, cut],
                          start=True, stop=True).then_inc(qkv_mm, 1)

            def take_turn(g, name):
                pe.wait_ge(turn_read, past(turn(g, name) - 1))

            def body(g):
                own, prev = has_group(g, 0), has_group(g, 1)
                for s in range(UPG):
                    U = UPG * g + s
                    t, half = s // HALVES, s % HALVES
                    if own:
                        if s == 0:
                            pe.wait_ge(xsT_ev, g + 1)
                            pe.wait_ge(w_dma, past(16 * 2 * (g + 1)))
                        for i in range(2):
                            project(g, s, i)
                    if prev and s == 7:
                        take_turn(g, "a1")
                        pe.matmul(SHARED[:, :], w1[:, P:2 * P], xnT[:, :], start=True, stop=True).then_inc(turn_mm, 1)
                    if alive(g, s, 3):
                        pe.wait_ge(o_done, past(U - 2))
                        if alive(g, s, 2):
                            pe.wait_ge(qT_ev, past(U - 1))
                        else:
                            pe.wait_ge(oT_ev, past(U - 3))
                        if prev and s == 7:
                            pe.wait_ge(gate_read, past(2 * g - 1))
                        for k in range(HP):
                            mm = pe.transpose(QT_BANK[:, k * P:(k + 1) * P], o[:, k * P:(k + 1) * P], ident)
                        mm.then_inc(oT_mm, 1)
                    if own:
                        project(g, s, 2)
                    if alive(g, s, 2):
                        pe.wait_ge(exp_done, past(U - 1))
                        pe.wait_ge(pT_ev, past(U - 2))
                        if prev and s == 0:
                            pe.wait_ge(down_read, ahead(g - 1))
                        if prev and s == 7:
                            pe.wait_ge(gate_read, past(2 * g))
                        for k in range(HP):
                            mm = pe.transpose(PT_BANK[:, k * P:(k + 1) * P], pr[:, s % 2, k * P:(k + 1) * P], ident)
                        mm.then_inc(pT_mm, 1)
                    if alive(g, s, 1):
                        pe.wait_ge(qn_done, past(U))
                        if alive(g, s, 3):
                            pe.wait_ge(oT_ev, past(U - 2))
                        else:
                            pe.wait_ge(qT_ev, past(U - 1))
                        for k in range(HP):
                            mm = pe.transpose(QT_BANK[:, k * P:(k + 1) * P], qkn[:, (s - 1) % 2, k * P:(k + 1) * P], ident)
                        mm.then_inc(qT_mm, 1)
                        pe.wait_ge(kn_done, past(U))
                        pe.wait_ge(kT_ev, past(2 * (U - 1)))
                        if prev and s == 7:
                            pe.wait_ge(u_done, ahead(3 * g - 2))
                        for k in range(HP):
                            mm = pe.transpose(KT_BANK[:, k * P:(k + 1) * P],
                                              qkn[:, (s - 1) % 2, UW + k * P:UW + (k + 1) * P], ident)
                        mm.then_inc(kT_mm, 1)
                    if prev and s == 6:
                        take_turn(g, "ln_t")
                        pe.wait_ge(f_xn, ahead(TPG * g))
                        for t_ in range(TPG):
                            mm = pe.transpose(SHARED[:, t_ * P:(t_ + 1) * P], xn[:, t_, :], ident)
                        mm.then_inc(turn_mm, 1)
                    if alive(g, s, 2):
                        gv = g if s >= 2 else g - 1
                        sv = (s - 2) % UPG
                        pe.wait_ge(pT_ev, past(U - 1))
                        pe.wait_ge(vw_dma[sv % 2], vw_count(gv, sv))
                        pe.wait_ge(o_done, past(U - 2))
                        for k in range(HP):
                            for w in range(NW):
                                mm = pe.matmul(heads(PV_BANK[WIN * w:WIN * (w + 1), k * P:(k + 1) * P]),
                                               pT[:, s % 2, k, WIN * w:WIN * (w + 1)],
                                               vw[:, sv % 2, w, :, k * DH:(k + 1) * DH], start=True, stop=True,
                                               tile_position=(0, WIN * w))
                        mm.then_inc(pv_mm, 1)
                    if s % 2 == 1 and alive(g, s, 4):
                        tile = (s - 4) // 2 % TPG
                        gy = g if s >= 4 else g - 1
                        name = f"y{tile}"
                        take_turn(g, name)
                        pe.wait_ge(oT_ev, past(U - 3))
                        for k in range(INNER // P):
                            mm = pe.matmul(SHARED[:, 0:C], oT[:, tile % 2, k, :], wo[:, (gy // B) % 2, k, :],
                                           start=(k == 0), stop=(k == INNER // P - 1))
                        mm.then_inc(turn_mm, 1)
                    if prev and s == 7:
                        pe.wait_ge(kT_ev, past(2 * U if own else 2 * UNITS))
                        pe.wait_ge(u_done, ahead(3 * g - 2))
                        pe.matmul(KT_BANK[:, :], w1[:, 2 * P:3 * P], xnT[:, :], start=True, stop=True).then_inc(a_mm, 1)
                    if alive(g, s, 1):
                        sk = (s - 1) % UPG
                        tk, hk = sk // HALVES, sk % HALVES
                        pe.wait_ge(qT_ev, past(U))
                        pe.wait_ge(kT_ev, past(2 * U))
                        pe.wait_ge(sub_done, past(U - 1))
                        pe.matmul(heads(SC_BANK[:, :]), ident_b[:, :],
                                  mask_b[:, min(tk, 1), :].unsqueeze(1).to_broadcast([P, HU, 2 * WIN]),
                                  start=True, stop=True)
                        for k in range(HP):
                            for w in range(NW):
                                c0 = P * tk + WIN * w
                                mm = pe.matmul(heads(SC_BANK[WIN * w:WIN * (w + 1), k * P:(k + 1) * P]),
                                               qT[:, sk % 2, k, WIN * w:WIN * (w + 1)],
                                               kB[:, HP * hk + k, :, c0:c0 + 2 * WIN],
                                               start=False, stop=True, tile_position=(0, WIN * w),
                                               skip_group_check=True)
                        mm.then_inc(score_mm, 1)
                    if own and s == 2:
                        take_turn(g, "shift_att")
                        b = (g + 1) % B
                        shift(lambda a, n: x[:, bass.ds(TPG * b + a, n), 64:C], turn_mm)
                    if prev and s == 4:
                        take_turn(g, "shift_ffn")
                        pe.wait_ge(att_res, past(TPG * g))
                        b = (g + B - 1) % B
                        shift(lambda a, n: x[:, bass.ds(TPG * b + a, n), 64:C], turn_mm)
                    if prev and s == 6:
                        pe.wait_ge(xnT_done, past(g))
                        pe.wait_ge(w1_dma, past(16 * g))
                        gate = lambda i: w1[:, DFF + i * P:DFF + (i + 1) * P]
                        take_turn(g, "gate0")
                        pe.matmul(SHARED[:, :], gate(0), xnT[:, :], start=True, stop=True).then_inc(turn_mm, 1)
                        if own:
                            pe.wait_ge(qT_ev, past(U))
                        else:
                            pe.wait_ge(oT_ev, UNITS)
                        pe.matmul(QT_BANK[:, :], gate(1), xnT[:, :], start=True, stop=True).then_inc(gate_mm, 1)
                        pe.wait_ge(pT_ev, past(U - 1 if own else UNITS))
                        pe.wait_ge(w1_pad, 1)
                        pe.matmul(PT_BANK[:, :], gate(2), xnT[:, :], start=True, stop=True).then_inc(gate_mm, 1)
                        pe.wait_ge(kT_ev, past(2 * U if own else 2 * UNITS))
                        pe.matmul(KT_BANK[:, :], w1[:, 0:P], xnT[:, :], start=True, stop=True).then_inc(a_mm, 1)
                    if own and s == 7:
                        take_turn(g, "x_t")
                        pe.wait_ge(xa_low, g + 1)
                        x_transposes(turn_mm)
                    if prev and s == 7:
                        if own:
                            pe.wait_ge(pT_ev, past(U - 1))
                        else:
                            pe.wait_ge(gate_read, past(2 * g))
                        pe.wait_ge(u_done, ahead(3 * g))
                        pe.wait_ge(w2_dma, past(32 * g))
                        for t_ in range(TPG):
                            for i, (r, m) in enumerate(BLK):
                                mm = pe.matmul(PT_BANK[:, t_ * P:(t_ + 1) * P], uT[0:m, i, t_ * P:(t_ + 1) * P],
                                               w2[0:m, i, :], start=(i == 0), stop=(i == len(BLK) - 1))
                        mm.then_inc(down_mm, 1)

            body(0)
            with pe.Fori(1, GROUPS) as g:
                body(g)
            body(GROUPS)

        @block.scalar
        def _(act):
            act.wait_ge(small_dma, 16 * 6)
            act.activation(tg[:, :], gcol[:, :], ACT.Tanh).then_inc(tanh_ready, 1)
            act.wait_ge(wxT_mm, 1)
            act.activation(wxT[:, :, :].rearrange("p a c -> p (a c)"), ps[0][:, :], ACT.Copy).then_inc(wxT_ev, 1)
            act.wait_ge(ctxT_mm, 1)
            act.activation(ctxT[:, :, :].rearrange("p b s -> p (b s)"), ps[1][:, 0:B * CTX], ACT.Copy).then_inc(ctxT_ev, 1)
            act.wait_ge(kx_mm, 1)
            act.activation(kxT[:, :, :].rearrange("p b s -> p (b s)"), ps[2][:, 0:B * CTX], ACT.Identity,
                           bias=bcol[:, 1:2]).then_inc(kx_ev, 1)
            act.wait_ge(vx_mm, 1)
            act.activation(vx[:, :, :].rearrange("p b c -> p (b c)"), ps[3][0:CTX, :], ACT.Copy).then_inc(vx_ev, 1)
            with act.Fori(0, B) as b:
                act.wait_ge(a_xnT, b + 1)
                act.activation(xnT[:, :], ps[0][:, :], ACT.Copy).then_inc(a_xnTev, 1)
                act.wait_ge(a_q, b + 1)
                act.activation(xsT[:, :], ps[1][:, :], ACT.Identity, bias=bcol[:, 0:1]).then_inc(a_qev, 1)
                act.wait_ge(a_sub, b + 1)
                act.activation(xf[:, :, 0:CTX], xf[:, :, 0:CTX], ACT.Exp, scale=float(C) ** -0.5).then_inc(a_exp, 1)
                act.wait_ge(a_pT, b + 1)
                act.activation(uT[0:CTX, 0, :], ps[3][0:CTX, :], ACT.Copy).then_inc(a_pTev, 1)
                act.wait_ge(a_rT, b + 1)
                act.activation(uT[:, 1, :], ps[5][:, :], ACT.Copy).then_inc(a_rTev, 1)
            act.wait_ge(b_x, ahead(B * TPG))
            act.activation(xa[:, :, 0:64], x[:, 0:TPG, 0:64], ACT.Copy).then_inc(p_low, 1)
            act.wait_ge(p_xT, 1)
            act.activation(xsT[:, :], SHARED[:, :], ACT.Copy).then_inc(xsT_ev, 1)
            act.wait_ge(zero_ready, 2)
            act.wait_ge(cst_ready, 5)
            act.preload_act_table_set("natural_log_exp_and_others")

            def exponentials(g, s):
                U = UPG * g + s
                if alive(g, s, 2):
                    act.wait_ge(sub_done, past(U - 1))
                    act.wait_ge(pT_mm, past(U - 3))
                    act.wait_ge(sum_done, past(U - 3))
                    act.activation(pr[:, s % 2, :], pr[:, s % 2, :], ACT.Exp).then_inc(exp_done, 1)

            def estimate(U):
                act.wait_ge(ssm_done, past(U))
                act.wait_ge(newton_done, past(2 * (U - 1)))
                act.activation(lnn[:, :], ssm[:, :], ACT.Ln, scale=LN_SHIFT).then_inc(ln_done, 1)
                act.wait_ge(ln_done, past(U))
                act.wait_ge(rn_done, past(U - 1))
                act.activation(seed[:, :], lnn[:, :], ACT.Exp, bias=shift_back[:, 0:1], scale=-0.5).then_inc(seed_done, 1)

            def body(g):
                own, prev = has_group(g, 0), has_group(g, 1)
                for s in range(UPG):
                    U = UPG * g + s
                    if own:
                        if s % 2 == 0 and s > 0:
                            estimate(U)
                        act.wait_ge(sq_done, past(U - 1))
                        act.wait_ge(cos_done, past(2 * (U - 1)))
                        act.wait_ge(sin_done, past(2 * (U - 1)))
                        act.wait_ge(qkv_mm, 3 * U + 1)
                        act.activation(qk[:, s % 2, 0:UW], QKV_BANKS[3 * s % 2][:, :], ACT.Copy).then_inc(qkv_ev, 1)
                    if alive(g, s, 1) and s % 2 == 1:
                        estimate(U)
                    if own:
                        act.wait_ge(qkv_mm, 3 * U + 2)
                        act.activation(qk[:, s % 2, UW:], QKV_BANKS[(3 * s + 1) % 2][:, :], ACT.Copy).then_inc(qkv_ev, 1)
                    if s > 0:
                        exponentials(g, s)
                    if own and s == 3:
                        act.wait_ge(turn_mm, turn(g, "shift_att"))
                        act.activation(xa[:, :, 64:C], heads(SHARED[:, 0:TPG * 64]), ACT.Copy).then_inc(turn_read, 1)
                    if prev and s == 5:
                        act.wait_ge(f_xn, ahead(TPG * (g - 1)))
                        act.wait_ge(turn_mm, turn(g, "shift_ffn"))
                        act.activation(xf[:, :, 64:C], heads(SHARED[:, 0:TPG * 64]), ACT.Copy).then_inc(turn_read, 1)
                    if alive(g, s, 3):
                        so = (s - 3) % UPG
                        to, ho = so // HALVES, so % HALVES
                        act.wait_ge(oT_mm, past(U - 2))
                        if alive(g, s, 3 + 2 * HALVES + ho):
                            act.wait_ge(att_res, past(TPG * g + (s - 3) // HALVES - 1))
                        act.activation(oT[:, to % 2, HP * ho:HP * ho + HP, :].rearrange("p k q -> p (k q)"),
                                       QT_BANK[:, :], ACT.Copy).then_inc(oT_ev, 1)
                    if alive(g, s, 2):
                        act.wait_ge(pT_mm, past(U - 1))
                        act.wait_ge(pv_mm, past(U - 3))
                        act.activation(pT[:, s % 2].rearrange("p k q -> p (k q)"), PT_BANK[:, :],
                                       ACT.Copy).then_inc(pT_ev, 1)
                    if alive(g, s, 1):
                        sk = (s - 1) % UPG
                        tk, hk = sk // HALVES, sk % HALVES
                        act.wait_ge(qT_mm, past(U))
                        act.wait_ge(score_mm, past(U - 2))
                        act.activation(qT[:, sk % 2].rearrange("p k q -> p (k q)"), QT_BANK[:, :],
                                       ACT.Copy).then_inc(qT_ev, 1)
                    if alive(g, s, 1):
                        act.wait_ge(kT_mm, past(U))
                        act.wait_ge(score_mm, past(U - 6))
                        for h in range(2):
                            act.activation(kB[64 * h:64 * h + 64, HP * hk:HP * hk + HP, h, WIN + P * tk:WIN + P * tk + P],
                                           KT_BANK[64 * h:64 * h + 64, :].rearrange("p (k q) -> p k q", q=P),
                                           ACT.Copy).then_inc(kT_ev, 1)
                    if prev and s == 6:
                        act.wait_ge(turn_mm, turn(g, "ln_t"))
                        act.wait_ge(cur_done, past(g))
                        act.activation(xnT[:, :], SHARED[:, :], ACT.Identity, bias=cur[:, 1:2],
                                       scale=cur[:, 0:1]).then_inc(turn_read, 1)
                        act.wait_ge(turn_read, turn(g, "ln_t"))
                        act.sem_inc(xnT_done, 1)
                    if own:
                        act.wait_ge(qkv_ev, 3 * U + 2)
                        act.wait_ge(ss_done, past(U))
                        act.activation(sq[:, :], qk[:, s % 2, :], ACT.Square).then_inc(sq_done, 1)
                    if own:
                        act.wait_ge(qkv_mm, 3 * U + 3)
                        if alive(g, s, 2):
                            s2, g2 = (s - 2) % UPG, (g if s >= 2 else g - 1)
                            act.wait_ge(vw_dma[s2 % 2], vw_count(g2, s2))
                        act.activation(vs[:, s % 4], QKV_BANKS[(3 * s + 2) % 2][:, :].rearrange(
                            "p (k h d) -> p h k d", h=2, d=DH), ACT.Copy).then_inc(qkv_ev, 1)
                    if own and s == 3:
                        act.wait_ge(turn_mm, turn(g, "shift_att"))
                        b = (g + 1) % B
                        src = x[:, bass.ds(TPG * b, TPG), 0:64]
                        act.activation(xa[:, :, 0:64], src, ACT.Copy).then_inc(xa_low, 1)
                    if prev and s == 4:
                        act.wait_ge(att_res, past(TPG * g))
                        b = (g + B - 1) % B
                        src = x[:, bass.ds(TPG * b, TPG), 0:64]
                        act.activation(xf[:, :, 0:64], src, ACT.Copy).then_inc(xf_low, 1)
                    if prev and s == 5:
                        act.wait_ge(f_var, past(g))
                        act.activation(f_tmp[:, :], vare[:, :], ACT.Ln).then_inc(f_ln, 1)
                        act.wait_ge(f_ln, past(g))
                        act.activation(f_seed[:, :], f_tmp[:, :], ACT.Exp, scale=-0.5).then_inc(f_seeded, 1)
                    if prev and s == 6:
                        act.preload_act_table(ACT.Gelu)
                        act.wait_ge(cur_done, past(g))
                        act.wait_ge(turn_mm, turn(g, "gate0"))
                        act.activation(uT[:, 0, :], SHARED[:, :], ACT.Gelu, bias=cur[:, 5:6]).then_inc(turn_read, 1)
                        for i, bank in ((1, QT_BANK), (2, PT_BANK)):
                            m = BLK[i][1]
                            act.wait_ge(gate_mm, past(2 * g - 2 + i))
                            act.activation(uT[0:m, i, :], bank[0:m, :], ACT.Gelu,
                                           bias=cur[0:m, 5 + i:6 + i]).then_inc(gate_read, 1)
                        act.preload_act_table_set("natural_log_exp_and_others")
                    if own and s == 7:
                        estimate(U + 1)
                        act.wait_ge(turn_mm, turn(g, "x_t"))
                        act.wait_ge(qkv_mm, 3 * U + 3)
                        act.activation(xsT[:, :], SHARED[:, :], ACT.Copy).then_inc(turn_read, 1)
                        act.wait_ge(turn_read, turn(g, "x_t"))
                        act.sem_inc(xsT_ev, 1)
                        exponentials(g + 1, 0)

            body(0)
            with act.Fori(1, GROUPS) as g:
                body(g)
            body(GROUPS)

        @block.vector
        def _(dve):
            for start in (f_xn, f_rstd, u_done, b_x, down_read):
                dve.sem_inc(start, 1)
            dve.memset(ones[:, :], 1.0).then_inc(cst_ready, 1)
            dve.memset(minus_half[:, :], -0.5).then_inc(cst_ready, 1)
            dve.memset(shift_back[:, :], 0.5 * float(np.log(LN_SHIFT))).then_inc(cst_ready, 1)
            dve.wait_ge(cst_dma, 16 * 9)
            dve.tensor_copy(mask_b[:, :, :], mask_f[:, :, :]).then_inc(cst_ready, 1)
            dve.tensor_copy(ident_b[:, :], ident).then_inc(cst_ready, 1)
            dve.wait_ge(tanh_ready, 1)
            dve.wait_ge(x_dma, 32)

            with dve.Fori(0, B) as b:
                def normalise(src, dst, stat, rst, done):
                    settle(dve)
                    for t in range(TPG):
                        dve.bn_stats(stats[:, t, :], src(t)).then_inc(stat, 1)
                    dve.wait_ge(stat, 2 * TPG * b + TPG)
                    settle(dve)
                    for t in range(TPG):
                        dve.bn_aggr(mv[:, t, :], stats[:, t, :]).then_inc(stat, 1)
                    dve.wait_ge(rst, 2 * b + 2)
                    dve.wait_ge(stat, 2 * TPG * b + 2 * TPG)
                    for t in range(TPG):
                        dve.tensor_scalar(dst(t), src(t), mv[:, t, 0:1], rstd[:, t:t + 1], ALU.subtract,
                                          ALU.mult).then_inc(done, 1)

                tile = lambda buf: (lambda t: buf[:, TPG * b + t, :])
                group = bass.ds(TPG * b, TPG)
                dve.wait_ge(b_x, ahead(TPG * b))
                normalise(tile(x1), lambda t: xn[:, t, :], a_stat, a_rstd, a_xn)
                dve.wait_ge(a_sc, b + 1)
                sc = heads(ps[2][:, :], P)[:, :, 0:CTX]
                dve.tensor_reduce(mx4[:, :], sc, AX.X, ALU.max).then_inc(a_mx, 1)
                dve.wait_ge(a_mx, b + 1)
                dve.tensor_tensor(xf[:, :, 0:CTX], sc, spread(mx4[:, :], CTX), ALU.subtract).then_inc(a_sub, 1)
                dve.wait_ge(a_exp, b + 1)
                dve.tensor_reduce(rs4[:, :], xf[:, :, 0:CTX], AX.X, ALU.add).then_inc(a_sum, 1)
                dve.wait_ge(a_sum, b + 1)
                dve.reciprocal(rr4[:, :], rs4[:, :]).then_inc(a_rec, 1)
                dve.wait_ge(a_rec, b + 1)
                dve.tensor_tensor(xf[:, :, 0:CTX], xf[:, :, 0:CTX], spread(rr4[:, :], CTX),
                                  ALU.mult).then_inc(a_pn, 1)
                dve.wait_ge(a_att, b + 1)
                dve.wait_ge(a_xn, 4 * b + 4)
                dve.tensor_tensor(xa[:, :, :], heads(ps[4][:, :], P), xn[:, :, :], ALU.add).then_inc(a_res, 1)
                dve.wait_ge(a_y, b + 1)
                dve.scalar_tensor_tensor(out=x1[:, group, :], in0=heads(ps[6][:, :], P), scalar=tg[:, 0:1],
                                         in1=x1[:, group, :], op0=ALU.mult, op1=ALU.add).then_inc(a_x1, 1)
                dve.wait_ge(a_x1, b + 1)
                normalise(tile(x1), tile(x), b_stat, b_rstd, b_x)
            dve.wait_ge(p_shift, 1)
            dve.tensor_copy(xa[:, :, 64:C], heads(SHARED[:, 0:TPG * 64])).then_inc(p_up, 1)

            def norms(g, s, U):
                dve.wait_ge(seed_done, past(U))
                dve.scalar_tensor_tensor(out=step[:, :], in0=seed[:, :], scalar=-0.5, in1=seed[:, :],
                                         op0=ALU.mult, op1=ALU.mult).then_inc(newton_done, 1)
                dve.wait_ge(newton_done, past(2 * U - 1))
                dve.tensor_tensor(step[:, :], step[:, :], ssm[:, :], ALU.mult).then_inc(newton_done, 1)
                dve.wait_ge(newton_done, past(2 * U))
                dve.wait_ge(kn_done, past(U - 1))
                dve.scalar_tensor_tensor(out=rn[:, :], in0=step[:, :], scalar=1.5, in1=seed[:, :],
                                         op0=ALU.add, op1=ALU.mult).then_inc(rn_done, 1)
                dve.wait_ge(rn_done, past(U))
                dve.wait_ge(rotq_done, past(U))
                q = heads(qkn[:, (s - 1) % 2, 0:UW])
                dve.tensor_tensor(q, q, spread(rn[:, 0:HU], DH), ALU.mult).then_inc(qn_done, 1)

            def head(g, s):
                U = UPG * g + s
                if s % 2 == 0 and alive(g, s, 1):
                    norms(g, s, U)
                if alive(g, s, 2):
                    dve.wait_ge(score_mm, past(U - 1))
                    dve.wait_ge(sub_done, past(U - 2))
                    dve.tensor_reduce(mx[:, :], heads(SC_BANK[:, :]), AX.X, ALU.max).then_inc(max_done, 1)
                    dve.wait_ge(max_done, past(U - 1))
                    dve.wait_ge(exp_done, past(U - 3))
                    dve.tensor_tensor(heads(pr[:, s % 2, :]), heads(SC_BANK[:, :]), spread(mx[:, :], DH),
                                      ALU.subtract).then_inc(sub_done, 1)
                if s % 2 == 1 and alive(g, s, 1):
                    norms(g, s, U)

            def body(g):
                own, prev = has_group(g, 0), has_group(g, 1)
                for s in range(UPG):
                    U = UPG * g + s
                    if s > 0:
                        head(g, s)
                    if prev and s == 7:
                        dve.wait_ge(a_mm, past(2 * g - 1))
                        dve.wait_ge(turn_read, turn(g, "gate0"))
                        dve.scalar_tensor_tensor(out=uT[:, 0, :], in0=KT_BANK[:, :], scalar=cur[:, 2:3],
                                                 in1=uT[:, 0, :], op0=ALU.add, op1=ALU.mult).then_inc(u_done, 1)
                    if own:
                        t = s // HALVES
                        if s == 0:
                            dve.wait_ge(table_ready, TPG + g)
                        dve.wait_ge(rotq_done, past(U))
                        dve.wait_ge(rotk_done, past(U))
                        for i in range(2):
                            dve.wait_ge(qkv_ev, 3 * U + i + 1)
                            table = tables[:, (g // B) % 2, t, 2 * DH * i:2 * DH * i + DH]
                            cut = slice(i * UW, (i + 1) * UW)
                            dve.tensor_tensor(heads(ra[:, cut]), heads(qk[:, s % 2, cut]),
                                              table.unsqueeze(1).to_broadcast([P, HU, DH]),
                                              ALU.mult).then_inc(cos_done, 1)
                    if prev and s == 5:
                        dve.wait_ge(f_xn, ahead(TPG * (g - 1)))
                        dve.wait_ge(turn_read, turn(g, "shift_ffn"))
                        dve.wait_ge(xf_low, past(g))
                        settle(dve)
                        for t_ in range(TPG):
                            dve.bn_stats(stats[:, t_, :], xf[:, t_, :]).then_inc(f_stat, 1)
                        dve.wait_ge(f_stat, past(TPG * g))
                        settle(dve)
                        for t_ in range(TPG):
                            dve.bn_aggr(mv[:, t_, :], stats[:, t_, :]).then_inc(f_aggr, 1)
                        dve.wait_ge(f_aggr, past(TPG * g))
                        dve.tensor_scalar(vare[:, :], mv[:, :, 1], LN_EPS, None, ALU.add).then_inc(f_var, 1)
                    if prev and s == 6:
                        dve.wait_ge(f_seeded, past(g))
                        dve.scalar_tensor_tensor(out=f_tmp[:, :], in0=f_seed[:, :], scalar=-0.5, in1=f_seed[:, :],
                                                 op0=ALU.mult, op1=ALU.mult).then_inc(f_newton, 1)
                        dve.wait_ge(f_newton, past(2 * g - 1))
                        dve.tensor_tensor(f_tmp[:, :], f_tmp[:, :], vare[:, :], ALU.mult).then_inc(f_newton, 1)
                        dve.wait_ge(f_newton, past(2 * g))
                        dve.scalar_tensor_tensor(out=rstd[:, :], in0=f_tmp[:, :], scalar=1.5, in1=f_seed[:, :],
                                                 op0=ALU.add, op1=ALU.mult).then_inc(f_rstd, 1)
                        dve.wait_ge(f_rstd, ahead(g))
                        for t_ in range(TPG):
                            dve.tensor_scalar(xn[:, t_, :], xf[:, t_, :], mv[:, t_, 0:1], rstd[:, t_:t_ + 1],
                                              ALU.subtract, ALU.mult).then_inc(f_xn, 1)
                    if prev and s == 7:
                        dve.wait_ge(turn_mm, turn(g, "a1"))
                        dve.wait_ge(gate_read, past(2 * g - 1))
                        dve.scalar_tensor_tensor(out=uT[:, 1, :], in0=SHARED[:, :], scalar=cur[:, 3:4],
                                                 in1=uT[:, 1, :], op0=ALU.add, op1=ALU.mult).then_inc(turn_read, 1)
                        dve.wait_ge(turn_read, turn(g, "a1"))
                        dve.sem_inc(u_done, 1)
                    if alive(g, s, 2):
                        dve.wait_ge(rec_done, past(U - 2))
                        dve.wait_ge(exp_done, past(U - 1))
                        dve.tensor_reduce(rs[:, :], heads(pr[:, s % 2, :]), AX.X, ALU.add).then_inc(sum_done, 1)
                        dve.wait_ge(sum_done, past(U - 1))
                        dve.reciprocal(rr[:, s % 2, :], rs[:, :]).then_inc(rec_done, 1)
                    if own:
                        dve.wait_ge(sin_done, 2 * U + 1)
                        dve.wait_ge(cos_done, 2 * U + 1)
                        dve.wait_ge(kT_mm, past(U - 1))
                        dve.tensor_tensor(qkn[:, s % 2, 0:UW], ra[:, 0:UW], rb[:, 0:UW], ALU.add).then_inc(rotq_done, 1)
                    if alive(g, s, 2):
                        dve.wait_ge(rec_done, past(U - 1))
                        dve.wait_ge(pv_mm, past(U - 1))
                        dve.wait_ge(oT_mm, past(U - 2))
                        dve.tensor_tensor(heads(o[:, :]), heads(PV_BANK[:, :]), spread(rr[:, s % 2, :], DH),
                                          ALU.mult).then_inc(o_done, 1)
                    if own:
                        dve.wait_ge(sq_done, U + 1)
                        dve.tensor_reduce(ss[:, :], heads(sq[:, :]), AX.X, ALU.add).then_inc(ss_done, 1)
                        dve.wait_ge(rn_done, past(U))
                        dve.wait_ge(ss_done, U + 1)
                        dve.tensor_scalar(ssm[:, :], ss[:, :], NORM_MIN ** 2, None, ALU.max).then_inc(ssm_done, 1)
                    if s % 2 == 1 and alive(g, s, 4):
                        tile = (s - 4) // 2 % TPG
                        gy = g if s >= 4 else g + B - 1
                        row = x[:, TPG * (gy % B) + tile, :]
                        dve.wait_ge(turn_mm, turn(g, f"y{tile}"))
                        dve.wait_ge(turn_read, past(turn(g, f"y{tile}") - 1))
                        dve.tensor_tensor(row, row, SHARED[:, 0:C], ALU.add).then_inc(turn_read, 1)
                        dve.wait_ge(turn_read, turn(g, f"y{tile}"))
                        dve.sem_inc(att_res, 1)
                    if prev and s == 7:
                        m = BLK[2][1]
                        dve.wait_ge(a_mm, past(2 * g))
                        dve.wait_ge(gate_read, past(2 * g))
                        dve.scalar_tensor_tensor(out=uT[0:m, 2, :], in0=KT_BANK[0:m, :], scalar=cur[0:m, 4:5],
                                                 in1=uT[0:m, 2, :], op0=ALU.add, op1=ALU.mult).then_inc(u_done, 1)
                    if own and s == 7:
                        head(g + 1, 0)
                    if prev and s == 7:
                        b = (g + B - 1) % B
                        rows = x[:, bass.ds(TPG * b, TPG), :]
                        dve.wait_ge(down_mm, past(g))
                        dve.wait_ge(b2_done, past(g))
                        dve.tensor_tensor(rows, rows, heads(PT_BANK[:, :], C), ALU.add).then_inc(down_read, 1)

            body(0)
            with dve.Fori(1, GROUPS) as g:
                body(g)
            body(GROUPS)
            dve.wait_ge(down_read, ahead(GROUPS))
            for b in range(B):
                rows = lambda buf: buf[:, TPG * b:TPG * (b + 1), :].rearrange("p t c -> p (t c)")
                dve.scalar_tensor_tensor(out=rows(x1), in0=rows(x), scalar=tg[:, 1:2], in1=rows(x1),
                                         op0=ALU.mult, op1=ALU.add).then_inc(fin, 1)

        @block.gpsimd
        def _(pool):
            pool.memset(cols[:, :, :], 0.0).then_inc(zero_ready, 1)
            pool.memset(w1[:, 2 * DFF:], 0.0).then_inc(w1_pad, 1)
            pool.memset(kB[:, :, :, :], 0.0).then_inc(zero_ready, 1)
            pool.wait_ge(cst_ready, 3)

            def inverse_root(b, stat, rst):
                pool.wait_ge(stat, 2 * TPG * b + 2 * TPG)
                settle(pool)
                pool.tensor_scalar(vare[:, :], mv[:, :, 1], LN_EPS, None, ALU.add).then_inc(rst, 1)
                pool.wait_ge(rst, 2 * b + 1)
                pool.tensor_tensor(rstd[:, :], vare[:, :], minus_half[:, 0:TPG], ALU.pow).then_inc(rst, 1)

            with pool.Fori(0, B) as b:
                inverse_root(b, a_stat, a_rstd)
                inverse_root(b, b_stat, b_rstd)

            pool.wait_ge(b_x, ahead(B * TPG))
            pool.memset(free, 0.0).then_inc(vw_zero, 1)
            pool.wait_ge(cst_dma, 16 * 9)
            for t in range(TPG):
                pool.tensor_tensor(tables[:, 0, t, :], rope[:, t, :], scales[:, 0, :], ALU.mult).then_inc(table_ready, 1)

            def add_b2(g):
                pool.wait_ge(turn_mm, turn(g, "shift_ffn"))
                pool.wait_ge(xf_low, past(g))
                settle(pool)
                b = (g + B - 1) % B
                rows = x[:, bass.ds(TPG * b, TPG), :]
                pool.tensor_tensor(rows, rows, b2r[:, (g - 1) // B, :].unsqueeze(1).to_broadcast([P, TPG, C]),
                                   ALU.add).then_inc(b2_done, 1)

            def body(g):
                own, prev = has_group(g, 0), has_group(g, 1)
                for s in range(UPG):
                    U = UPG * g + s
                    if own:
                        t = s // HALVES
                        if s == 0:
                            pool.wait_ge(table_ready, TPG + g)
                        for i in range(2):
                            pool.wait_ge(qkv_ev, 3 * U + i + 1)
                            pool.wait_ge(rotq_done, past(U))
                            pool.wait_ge(rotk_done, past(U))
                            settle(pool)
                            table = tables[:, (g // B) % 2, t, 2 * DH * i + DH:2 * DH * (i + 1)]
                            cut = slice(i * UW, (i + 1) * UW)
                            halves = lambda ap: ap.rearrange("p (h a d) -> p h a d", a=2, d=DH // 2)
                            pool.tensor_tensor(
                                halves(rb[:, cut]), halves(qk[:, s % 2, cut])[:, :, ::-1, :],
                                table.rearrange("p (a d) -> p a d", a=2).unsqueeze(1).to_broadcast([P, HU, 2, DH // 2]),
                                ALU.mult).then_inc(sin_done, 1)
                        pool.wait_ge(cos_done, 2 * U + 2)
                        pool.wait_ge(sin_done, 2 * U + 2)
                        pool.wait_ge(kT_mm, past(U - 1))
                        settle(pool)
                        pool.tensor_tensor(qkn[:, s % 2, UW:], ra[:, UW:], rb[:, UW:], ALU.add).then_inc(rotk_done, 1)
                        if prev and s == 5:
                            add_b2(g)
                        pool.wait_ge(rotk_done, U + 1)
                        pool.wait_ge(rn_done, U + 1)
                        settle(pool)
                        k = heads(qkn[:, s % 2, UW:])
                        pool.tensor_tensor(k, k, spread(rn[:, HU:], DH), ALU.mult).then_inc(kn_done, 1)
                    if prev and s == 4:
                        if isinstance(g, int):
                            pool.wait_ge(cols_dma, 16 * 9)
                        pool.wait_ge(u_done, ahead(3 * (g - 1)))
                        pool.tensor_copy(cur[:, :], cols[:, (g - 1) // B, :]).then_inc(cur_done, 1)
                    if prev and not own and s == 5:
                        add_b2(g)
                    if own and s == 7:
                        layer, place, part = (g // B + 1) % DEPTH, (g // B + 1) % 2, g % B
                        pool.wait_ge(cos_done, past(2 * UPG * g))
                        settle(pool)
                        pool.tensor_tensor(tables[:, place, part, :], rope[:, part, :], scales[:, layer, :],
                                           ALU.mult).then_inc(table_ready, 1)

            pool.wait_ge(cols_dma, 16 * 9)
            body(0)
            with pool.Fori(1, GROUPS) as g:
                body(g)
            body(GROUPS)


_INS = ["x", "ctx_1024", "g_xattn", "g_ffn", "L0_xattn_Wq", "L0_xattn_bq", "L0_xattn_Wk", "L0_xattn_bk", "L0_xattn_Wv",
        "L0_xattn_bv", "L0_xattn_Wo", "L0_xattn_bo", "L0_ffn_Wqkv", "L0_ffn_q_scale", "L0_ffn_k_scale", "L0_ffn_Wo",
        "L0_ffn_ln_g", "L0_ffn_ln_b", "L0_ffn_W1", "L0_ffn_b1", "L0_ffn_W2", "L0_ffn_b2"]


def kernel(**inputs):
    import numpy as _np
    import concourse.bacc as _bacc
    from concourse import mybir as _mybir
    from concourse.bass_utils import run_bass_kernel_spmd as _run

    nc = _bacc.Bacc("TRN2", target_bir_lowering=False, num_devices=1)
    arrays, args = {}, []
    given = [(n, _np.ascontiguousarray(inputs[n])) for n in _INS]
    given += list(zip(("rope", "mats", "mask"), constants()))
    for name, a in given:
        arrays[f"in_{name}_dram"] = a
        args.append(nc.dram_tensor(f"in_{name}_dram", a.shape, _mybir.dt.from_np(a.dtype), kind="ExternalInput").ap())
    out = nc.dram_tensor("out_0_dram", (B, N, C), _mybir.dt.float32, kind="ExternalOutput").ap()
    build(nc, *args, out)
    r = _run(nc, [arrays], core_ids=[0])
    return r.results[0]["out_0_dram"]
```

```python
from contextlib import ExitStack

import numpy as np

import concourse.bass as bass
from concourse import mybir

F32 = mybir.dt.float32
BF16 = mybir.dt.bfloat16
ALU = mybir.AluOpType
ACT = mybir.ActivationFunctionType
AX = mybir.AxisListType

P = 128
B, N, C = 4, 512, 128
CTX = 77
DEPTH, HEADS, DH, WIN = 6, 16, 64, 32
INNER = HEADS * DH
DFF = 341
TPG = N // P
GROUPS = DEPTH * B
HALVES = 2
UPG = TPG * HALVES
UNITS = GROUPS * UPG
HU = HEADS // HALVES
HP = HU // 2
UW = HU * DH
NW = P // WIN
BLK = [(0, 128), (128, 128), (256, DFF - 256)]
LN_EPS = 1e-5
NORM_MIN = 1e-12
LN_SHIFT = 2.0 ** 16


TURNS = ["y2", "shift_att", "y3", "shift_ffn", "y0", "ln_t", "gate0", "a1", "y1", "x_t"]
FIRST_TURNS = ["shift_att", "y0", "y1", "x_t"]
LAST_TURNS = ["y2", "y3", "shift_ffn", "ln_t", "gate0", "a1"]


def turn(g, name):
    if isinstance(g, int) and g == 0:
        return FIRST_TURNS.index(name) + 1
    lacking = len(TURNS) - len(FIRST_TURNS)
    order = LAST_TURNS if isinstance(g, int) and g == GROUPS else TURNS
    return len(TURNS) * g - lacking + order.index(name) + 1


def constants():
    f = np.float32
    half = np.arange(0, DH, 2, dtype=f)
    inv_freq = (f(1.0) / f(10000.0) ** (half / f(DH))).astype(f)
    t = np.arange(N, dtype=f)
    freqs = t[:, None] * inv_freq[None, :]
    base = (half + f(0.4 * DH)) / f(1.4 * DH)
    power = (t - f(N // 2)) / f(WIN // 2)
    scale = base[None, :] ** power[:, None]
    inv = f(1.0) / scale
    cos, sin = np.cos(freqs), np.sin(freqs)
    both = lambda a, b: np.concatenate([a, b], 1)
    qk_scale = f(8.0)
    tables = np.concatenate([
        both(cos * scale, cos * scale) * qk_scale, both(-sin * scale, sin * scale) * qk_scale,
        both(cos * inv, cos * inv), both(-sin * inv, sin * inv)], 1).astype(f)
    rope = tables.reshape(TPG, P, 4 * DH).transpose(1, 0, 2)
    ident = np.eye(P, dtype=f)
    down1 = np.eye(P, k=1, dtype=f)
    wrap = np.zeros((P, P), f)
    wrap[P - 1, 0] = 1.0
    i = np.arange(P)[:, None] % WIN
    j = np.arange(2 * WIN)[None, :]
    seen = (j >= i) & (j <= i + WIN)
    first = seen & ((np.arange(P)[:, None] >= WIN) | (j >= WIN))
    mask = np.where(np.stack([first, seen], 1), f(0.0), f(-3.0e38)).astype(f)
    return (np.ascontiguousarray(rope), np.concatenate([ident, down1, wrap], 1),
            np.ascontiguousarray(mask))


def build(nc, x_in, ctx_in, g_xattn, g_ffn, Wq, bq, Wk, bk, Wv, bv, Wo_x, bo, Wqkv, q_scale, k_scale,
          Wo, ln_g, ln_b, W1, b1, W2, b2, rope_in, mats_in, mask_in, out):
    ctx = ExitStack()
    with ctx:
        def sb(name, shape, dt=F32):
            return ctx.enter_context(nc.sbuf_tensor(name, shape, dt))

        def sem(name):
            return ctx.enter_context(nc.semaphore(name))

        ps = [ctx.enter_context(nc.psum_tensor(f"bank{i}", [P, 512], F32)) for i in range(8)]
        QKV_BANKS, QT_BANK, KT_BANK, SC_BANK, PT_BANK, PV_BANK, SHARED = ps[0:2], ps[2], ps[3], ps[4], ps[5], ps[6], ps[7]

        mats = sb("mats", [P, 3 * P])
        ident, down1, wrap = mats[:, 0:P], mats[:, P:2 * P], mats[:, 2 * P:3 * P]
        mask_f = sb("mask_f", [P, 2, 2 * WIN])
        mask_b = sb("mask_b", [P, 2, 2 * WIN], BF16)
        ident_b = sb("ident_b", [P, P], BF16)
        rope = sb("rope", [P, TPG, 4 * DH])
        scales = sb("scales", [P, DEPTH, 4 * DH])
        tables = sb("tables", [P, 2, TPG, 4 * DH])
        wqkv = sb("wqkv", [P, 2, 3 * INNER])
        wo = sb("wo", [P, 2, INNER // P, C])
        w1 = sb("w1", [P, DFF + len(BLK) * P])
        w2 = sb("w2", [P, len(BLK), C])
        b2r = sb("b2r", [P, DEPTH, C])
        cols = sb("cols", [P, DEPTH, 8])
        cur = sb("cur", [P, 8])
        x1 = sb("x1", [P, B * TPG, C])
        x = sb("x", [P, B * TPG, C])
        xa = sb("xa", [P, TPG, C])
        xsT = sb("xsT", [P, N])
        xf = sb("xf", [P, TPG, C])
        xn = sb("xn", [P, TPG, C])
        xnT = sb("xnT", [P, N])
        uT = sb("uT", [P, len(BLK), N])
        stats = sb("stats", [P, TPG, 6])
        mv = sb("mv", [P, TPG, 2])
        vare = sb("vare", [P, TPG])
        rstd = sb("rstd", [P, TPG])
        f_tmp = sb("f_tmp", [P, TPG])
        f_seed = sb("f_seed", [P, TPG])
        minus_half = sb("minus_half", [P, 2 * HU])
        qk = sb("qk", [P, 2, 2 * UW])
        sq = sb("sq", [P, 2 * UW])
        ra = sb("ra", [P, 2 * UW])
        rb = sb("rb", [P, 2 * UW])
        qkn = sb("qkn", [P, 2, 2 * UW])
        ss = sb("ss", [P, 2 * HU])
        ssm = sb("ssm", [P, 2 * HU])
        lnn = sb("lnn", [P, 2 * HU])
        seed = sb("seed", [P, 2 * HU])
        step = sb("step", [P, 2 * HU])
        rn = sb("rn", [P, 2 * HU])
        shift_back = sb("shift_back", [P, 1])
        qT = sb("qT", [P, 2, HP, P])
        kB = sb("kB", [P, HALVES * HP, 2, WIN + N])
        vs = sb("vs", [P, 4, 2, HP, DH])
        vw = sb("vw", [P, 2, NW, 2, HP * DH])
        pr = sb("pr", [P, 2, UW])
        pT = sb("pT", [P, 2, HP, P])
        o = sb("o", [P, UW])
        oT = sb("oT", [P, 2, INNER // P, P])
        mx = sb("mx", [P, HU])
        rs = sb("rs", [P, HU])
        rr = sb("rr", [P, 2, HU])
        free = vw[:, :, :, :, :].rearrange("p k w h n -> p (k w h n)")

        def take(start, groups, width):
            return free[:, start:start + groups * width].rearrange("p (a c) -> p a c", c=width)

        wx_in, wxT = take(0, 4, C), take(512, 4, C)
        ctx_sb, vx = take(1024, B, C)[0:CTX], take(1536, B, C)[0:CTX]
        ctxT, kxT = take(2048, B, CTX), take(2560, B, CTX)
        bcol = sb("bcol", [P, 2])
        brow = sb("brow", [1, 2, C])
        ones = sb("ones", [1, P])
        gcol = sb("gcol", [P, 2])
        tg = sb("tg", [P, 2])
        quad = lambda ap, n=C: ap.rearrange("p (t c) -> p t c", c=n)
        flat = lambda ap: ap.rearrange("p k q -> p (k q)")
        xn_x = [quad(qk[:, j, 0:UW]) for j in range(2)]
        xnT_x = [qk[:, j, UW:] for j in range(2)]
        q_x = [qkn[:, j, 0:UW] for j in range(2)]
        res_x = [quad(qkn[:, j, UW:]) for j in range(2)]
        pr_x = [quad(pr[:, j, 0:TPG * CTX], CTX) for j in range(2)]
        pT_x = [flat(pT[:, j]) for j in range(2)]
        rT_x = [flat(qT[:, j]) for j in range(2)]
        small = lambda j, start, n: sq[:, 64 * j + start:64 * j + start + n]
        stats_x = [quad(small(j, 0, 6 * TPG), 6) for j in range(2)]
        mv_x = [quad(small(j, 24, 2 * TPG), 2) for j in range(2)]
        vare_x, rstd_x, mx_x, rs_x, rr_x = ([small(j, 32 + 4 * i, TPG) for j in range(2)] for i in range(5))

        x_dma = sem("x_dma")
        mats_dma = sem("mats_dma")
        cst_dma = sem("cst_dma")
        small_dma = sem("small_dma")
        wx_dma = sem("wx_dma")
        w_dma = sem("w_dma")
        w1_dma = sem("w1_dma")
        w2_dma = sem("w2_dma")
        cols_dma = sem("cols_dma")
        out_dma = sem("out_dma")
        cst_ready = sem("cst_ready")
        settled = sem("settled")
        zero_ready = sem("zero_ready")
        w1_pad = sem("w1_pad")
        vw_zero = sem("vw_zero")
        tanh_ready = sem("tanh_ready")
        table_ready = sem("table_ready")
        wxT_mm = sem("wxT_mm")
        wxT_ev = sem("wxT_ev")
        ctxT_mm = sem("ctxT_mm")
        ctxT_ev = sem("ctxT_ev")
        kx_mm = sem("kx_mm")
        kx_ev = sem("kx_ev")
        vx_mm = sem("vx_mm")
        vx_ev = sem("vx_ev")
        a_stat = sem("a_stat")
        a_rstd = sem("a_rstd")
        a_xn = sem("a_xn")
        a_xnT = sem("a_xnT")
        a_xnTev = sem("a_xnTev")
        a_q = sem("a_q")
        a_qev = sem("a_qev")
        a_sc = sem("a_sc")
        a_mx = sem("a_mx")
        a_sub = sem("a_sub")
        a_exp = sem("a_exp")
        a_sum = sem("a_sum")
        a_rec = sem("a_rec")
        a_pn = sem("a_pn")
        a_pT = sem("a_pT")
        a_pTev = sem("a_pTev")
        a_att = sem("a_att")
        a_res = sem("a_res")
        a_rT = sem("a_rT")
        a_rTev = sem("a_rTev")
        a_y = sem("a_y")
        a_x1 = sem("a_x1")
        b_stat = sem("b_stat")
        b_rstd = sem("b_rstd")
        b_x = sem("b_x")
        p_shift = sem("p_shift")
        p_up = sem("p_up")
        p_low = sem("p_low")
        p_xT = sem("p_xT")
        qkv_mm = sem("qkv_mm")
        qkv_ev = sem("qkv_ev")
        sq_done = sem("sq_done")
        cos_done = sem("cos_done")
        sin_done = sem("sin_done")
        ss_done = sem("ss_done")
        ssm_done = sem("ssm_done")
        ln_done = sem("ln_done")
        seed_done = sem("seed_done")
        newton_done = sem("newton_done")
        rn_done = sem("rn_done")
        rotq_done = sem("rotq_done")
        rotk_done = sem("rotk_done")
        qn_done = sem("qn_done")
        kn_done = sem("kn_done")
        qT_mm = sem("qT_mm")
        kT_mm = sem("kT_mm")
        qT_ev = sem("qT_ev")
        kT_ev = sem("kT_ev")
        score_mm = sem("score_mm")
        max_done = sem("max_done")
        sub_done = sem("sub_done")
        exp_done = sem("exp_done")
        sum_done = sem("sum_done")
        rec_done = sem("rec_done")
        pT_mm = sem("pT_mm")
        pT_ev = sem("pT_ev")
        pv_mm = sem("pv_mm")
        o_done = sem("o_done")
        oT_mm = sem("oT_mm")
        oT_ev = sem("oT_ev")
        att_res = sem("att_res")
        turn_mm = sem("turn_mm")
        turn_read = sem("turn_read")
        xa_low = sem("xa_low")
        xsT_ev = sem("xsT_ev")
        xf_low = sem("xf_low")
        f_stat = sem("f_stat")
        f_aggr = sem("f_aggr")
        f_var = sem("f_var")
        f_rstd = sem("f_rstd")
        f_xn = sem("f_xn")
        b2_done = sem("b2_done")
        cur_done = sem("cur_done")
        xnT_done = sem("xnT_done")
        f_ln = sem("f_ln")
        f_seeded = sem("f_seeded")
        f_newton = sem("f_newton")
        gate_mm = sem("gate_mm")
        gate_read = sem("gate_read")
        a_mm = sem("a_mm")
        down_mm = sem("down_mm")
        down_read = sem("down_read")
        u_done = sem("u_done")
        fin = sem("fin")
        vw_dma = [sem(f"vw_dma{i}") for i in range(2)]

        def past(count):
            return max(count, 0) if isinstance(count, int) else count

        def ahead(count):
            return count + 1

        def settle(eng):
            eng.sem_inc(settled, 1)

        def alive(g, s, lag):
            if isinstance(g, int) and g == 0:
                return s >= lag
            if isinstance(g, int) and g == GROUPS:
                return s < lag
            return True

        def has_group(g, back):
            if isinstance(g, int) and g == 0:
                return back == 0
            if isinstance(g, int) and g == GROUPS:
                return back == 1
            return True

        def heads(ap, d=DH):
            return ap.rearrange("p (h d) -> p h d", d=d)

        def spread(ap, n):
            return ap.unsqueeze(2).to_broadcast([P, ap.shape[1], n])

        def vw_count(g, s):
            per_unit = 2 * (NW + 1)
            per_group = per_unit * TPG - 2
            return 16 * (per_group * g + per_unit * (s // HALVES + 1) - 2)

        block = ctx.enter_context(nc.Block())

        @block.sync
        def _(sp):
            xt = x_in.rearrange("b (t p) c -> p (b t) c", p=P)
            half = B * TPG // 2
            sp.dma_start(x1[:, 0:half, :], xt[:, 0:half, :]).then_inc(x_dma, 16)
            sp.dma_start(mats[:, :], mats_in).then_inc(mats_dma, 16)
            sp.dma_start(mask_f[:, :, :], mask_in).then_inc(mats_dma, 16)
            sp.dma_start(ctx_sb[:, :, :], ctx_in.rearrange("b s c -> s b c")).then_inc(wx_dma, 16)
            for i, w in enumerate((Wq, Wk, Wv, Wo_x)):
                sp.dma_start(wx_in[:, i, :], w).then_inc(wx_dma, 16)
            sp.dma_start(bcol[:, 0:1], bq.unsqueeze(1)).then_inc(small_dma, 16)
            sp.dma_start(bcol[:, 1:2], bk.unsqueeze(1)).then_inc(small_dma, 16)
            sp.dma_start(brow[:, 0, :], bv.unsqueeze(0)).then_inc(small_dma, 16)
            sp.dma_start(brow[:, 1, :], bo.unsqueeze(0)).then_inc(small_dma, 16)
            sp.dma_start(gcol[:, 0:1], g_xattn.unsqueeze(0).to_broadcast([P, 1])).then_inc(small_dma, 16)
            sp.dma_start(gcol[:, 1:2], g_ffn.unsqueeze(0).to_broadcast([P, 1])).then_inc(small_dma, 16)
            sp.dma_start(x1[:, half:, :], xt[:, half:, :]).then_inc(x_dma, 16)
            sp.dma_start(rope[:, :, :], rope_in).then_inc(cst_dma, 16)
            h = DH // 2
            for i, s in enumerate((q_scale, k_scale)):
                for dst, src in ((0, 0), (DH, h), (DH + h, 0)):
                    n = DH if dst == 0 else h
                    sp.dma_start(scales[:, :, 2 * DH * i + dst:2 * DH * i + dst + n],
                                 s[:, src:src + n].unsqueeze(0).to_broadcast([P, DEPTH, n])).then_inc(cst_dma, 16)
            sp.dma_start(wqkv[:, 0, :], Wqkv[0]).then_inc(w_dma, 16)
            sp.dma_start(wo[:, 0, :, :], Wo[0].rearrange("(k p) n -> p k n", p=P)).then_inc(w_dma, 16)
            sp.dma_start(w1[:, 0:2 * DFF], W1[0]).then_inc(w1_dma, 16)
            def second_weights(layer):
                sp.dma_start(w2[:, 0:2, :], W2[layer, 0:2 * P, :].rearrange("(i p) n -> p i n", p=P)).then_inc(w2_dma, 16)
                sp.dma_start(w2[0:DFF - 2 * P, 2, :], W2[layer, 2 * P:DFF, :]).then_inc(w2_dma, 16)

            second_weights(0)
            sp.dma_start(b2r[:, :, :], b2.unsqueeze(0).to_broadcast([P, DEPTH, C])).then_inc(cols_dma, 16)
            sp.wait_ge(zero_ready, 1)
            with nc.allow_non_contiguous_dma(reason="a few bias columns"):
                sp.dma_start(cols[:, :, 0], ln_g.rearrange("l p -> p l")).then_inc(cols_dma, 16)
                sp.dma_start(cols[:, :, 1], ln_b.rearrange("l p -> p l")).then_inc(cols_dma, 16)
                for half in range(2):
                    for i, (r, m) in enumerate(BLK):
                        sp.dma_start(cols[0:m, :, 2 + 3 * half + i],
                                     b1[:, DFF * half + r:DFF * half + r + m].rearrange("l p -> p l")
                                     ).then_inc(cols_dma, 16)

            def v_copies(g, s):
                U = UPG * g + s
                sp.wait_ge(qkv_ev, 3 * U + 3)
                settle(sp)
                sp.wait_ge(pv_mm, past(U - 1))
                sp.wait_ge(vw_zero, 1)
                k = s % 2
                src = vs[:, s % 4]
                for h in range(2):
                    for w in range(NW):
                        rows = lambda ap: ap.rearrange("p a d -> p (a d)")
                        if w > 0:
                            sp.dma_start(vw[64 * h:64 * h + 64, k, w, h, :],
                                         rows(src[WIN * (w - 1):WIN * (w + 1), h])).then_inc(vw_dma[k], 16)
                            continue
                        sp.dma_start(vw[64 * h + WIN:64 * h + 64, k, w, h, :],
                                     rows(src[0:WIN, h])).then_inc(vw_dma[k], 16)
                        if s // HALVES > 0:
                            sp.dma_start(vw[64 * h:64 * h + WIN, k, w, h, :],
                                         rows(vs[P - WIN:P, (s - 2) % 4, h])).then_inc(vw_dma[k], 16)

            def next_weights(g):
                q = INNER * 3 // 4
                layer, part = (g // B + 1) % DEPTH, g % B
                place = (g // B + 1) % 2
                sp.dma_start(wqkv[:, place, bass.ds(part * q, q)], Wqkv[layer, :, bass.ds(part * q, q)]).then_inc(w_dma, 16)
                sp.dma_start(wo[:, place, bass.ds(2 * part, 2), :],
                             Wo[layer, bass.ds(2 * P * part, 2 * P), :].rearrange("(k p) n -> p k n", p=P)
                             ).then_inc(w_dma, 16)

            def body(g):
                for s in range(UPG):
                    v_copies(g, s)
                    if s == 4:
                        sp.wait_ge(qkv_mm, past(3 * UPG * g))
                        if has_group(g, 1):
                            sp.wait_ge(turn_mm, turn(g, "y3"))
                        settle(sp)
                        next_weights(g)
                if has_group(g, 1):
                    sp.wait_ge(a_mm, past(2 * g))
                    settle(sp)
                    sp.dma_start(w1[:, 0:2 * DFF], W1[g // B]).then_inc(w1_dma, 16)
                    sp.wait_ge(down_mm, past(g))
                    settle(sp)
                    second_weights(g // B)

            body(0)
            with sp.Fori(1, GROUPS) as g:
                body(g)
            ot = out.rearrange("b (t p) c -> p (b t) c", p=P)
            for b in range(B):
                sp.wait_ge(fin, b + 1)
                sp.dma_start(ot[:, TPG * b:TPG * (b + 1), :], x1[:, TPG * b:TPG * (b + 1), :]).then_inc(out_dma, 16)
            sp.wait_ge(out_dma, 16 * B)

        @block.tensor
        def _(pe):
            pe.wait_ge(mats_dma, 16 * 2)
            pe.wait_ge(wx_dma, 16 * 5)
            for i in range(4):
                mm = pe.transpose(ps[0][:, i * C:(i + 1) * C], wx_in[:, i, :], ident)
            mm.then_inc(wxT_mm, 1)
            for b in range(B):
                mm = pe.transpose(ps[1][:, b * CTX:(b + 1) * CTX], ctx_sb[:, b, :], ident[0:CTX, 0:CTX])
            mm.then_inc(ctxT_mm, 1)
            pe.wait_ge(wxT_ev, 1)
            pe.wait_ge(ctxT_ev, 1)
            pe.wait_ge(cst_ready, 5)
            pe.matmul(ps[2][:, 0:B * CTX], wxT[:, 1, :], ctxT[:, :, :].rearrange("p b s -> p (b s)"),
                      start=True, stop=True).then_inc(kx_mm, 1)
            pe.wait_ge(small_dma, 16 * 6)
            for b in range(B):
                o_ = ps[3][0:CTX, b * C:(b + 1) * C]
                pe.matmul(o_, ones[0:1, 0:CTX], brow[0:1, 0, :], start=True, stop=False)
                mm = pe.matmul(o_, ctxT[:, b, :], wxT[:, 2, :], start=False, stop=True)
            mm.then_inc(vx_mm, 1)
            pe.wait_ge(kx_ev, 1)
            pe.wait_ge(vx_ev, 1)
            with pe.Fori(0, B // 2) as pair:
                for j in range(2):
                    pe.wait_ge(a_xn, 4 * (2 * pair + j) + 4)
                    for t in range(TPG):
                        mm = pe.transpose(ps[4 * j][:, t * P:(t + 1) * P], xn_x[j][:, t, :], ident)
                    mm.then_inc(a_xnT, 1)
                for j in range(2):
                    pe.wait_ge(a_xnTev, 2 * pair + j + 1)
                    pe.matmul(ps[4 * j + 1][:, :], wxT[:, 0, :], xnT_x[j], start=True, stop=True).then_inc(a_q, 1)
                for j in range(2):
                    pe.wait_ge(a_qev, 2 * pair + j + 1)
                    for t in range(TPG):
                        mm = pe.matmul(ps[4 * j + 2][:, t * P:t * P + CTX], q_x[j][:, t * P:(t + 1) * P],
                                       kxT[:, 2 * pair + j, :], start=True, stop=True)
                    mm.then_inc(a_sc, 1)
                for j in range(2):
                    pe.wait_ge(a_pn, 2 * pair + j + 1)
                    for t in range(TPG):
                        mm = pe.transpose(ps[4 * j + 3][0:CTX, t * P:(t + 1) * P], pr_x[j][:, t, :], ident)
                    mm.then_inc(a_pT, 1)
                for j in range(2):
                    pe.matmul(heads(ps[4 * j + 2][:, :], C), ones[0:1, :],
                              brow[0:1, 1, :].unsqueeze(1).to_broadcast([1, TPG, C]), start=True, stop=True)
                for j in range(2):
                    pe.wait_ge(a_pTev, 2 * pair + j + 1)
                    for t in range(TPG):
                        mm = pe.matmul(ps[4 * j][:, t * P:(t + 1) * P], pT_x[j][0:CTX, t * P:(t + 1) * P],
                                       vx[:, 2 * pair + j, :], start=True, stop=True)
                    mm.then_inc(a_att, 1)
                for j in range(2):
                    pe.wait_ge(a_res, 2 * pair + j + 1)
                    for t in range(TPG):
                        mm = pe.transpose(ps[4 * j + 1][:, t * P:(t + 1) * P], res_x[j][:, t, :], ident)
                    mm.then_inc(a_rT, 1)
                for j in range(2):
                    pe.wait_ge(a_rTev, 2 * pair + j + 1)
                    for t in range(TPG):
                        mm = pe.matmul(ps[4 * j + 2][:, t * P:(t + 1) * P], rT_x[j][:, t * P:(t + 1) * P], wxT[:, 3, :],
                                       start=False, stop=True, skip_group_check=True)
                    mm.then_inc(a_y, 1)

            def shift(xg, inc):
                pe.matmul(SHARED[:, 0:TPG * 64], down1, xg(0, TPG), start=True, stop=True)
                pe.matmul(SHARED[:, 64:TPG * 64], wrap, xg(0, TPG - 1), start=False, stop=True,
                          skip_group_check=True).then_inc(inc, 1)

            def x_transposes(inc):
                for t in range(TPG):
                    mm = pe.transpose(SHARED[:, t * P:(t + 1) * P], xa[:, t, :], ident)
                mm.then_inc(inc, 1)

            pe.wait_ge(b_x, ahead(B * TPG))
            shift(lambda a, n: x[:, a:a + n, 64:C], p_shift)
            pe.wait_ge(p_up, 1)
            pe.wait_ge(p_low, 1)
            x_transposes(p_xT)

            def project(g, s, i):
                n, t, half = 3 * (UPG * g + s) + i, s // HALVES, s % HALVES
                pe.wait_ge(qkv_ev, past(n - 1))
                cut = slice(i * INNER + half * UW, i * INNER + half * UW + UW)
                pe.matmul(QKV_BANKS[(3 * s + i) % 2][:, :],
                          xsT[:, t * P:(t + 1) * P], wqkv[:, (g // B) % 2, cut],
                          start=True, stop=True).then_inc(qkv_mm, 1)

            def take_turn(g, name):
                pe.wait_ge(turn_read, past(turn(g, name) - 1))

            def transpose_o(g, s):
                U = UPG * g + s
                prev = has_group(g, 1)
                if alive(g, s, 3):
                    pe.wait_ge(o_done, past(U - 2))
                    if alive(g, s, 2):
                        pe.wait_ge(qT_ev, past(U - 1))
                    else:
                        pe.wait_ge(oT_ev, past(U - 3))
                    if prev and s == 7:
                        pe.wait_ge(gate_read, past(2 * g - 1))
                    for k in range(HP):
                        mm = pe.transpose(QT_BANK[:, k * P:(k + 1) * P], o[:, k * P:(k + 1) * P], ident)
                    mm.then_inc(oT_mm, 1)

            def transpose_p(g, s):
                U = UPG * g + s
                prev = has_group(g, 1)
                if alive(g, s, 2):
                    pe.wait_ge(exp_done, past(U - 1))
                    pe.wait_ge(pT_ev, past(U - 2))
                    if prev and s == 0:
                        pe.wait_ge(down_read, ahead(g - 1))
                    if prev and s == 7:
                        pe.wait_ge(gate_read, past(2 * g))
                    for k in range(HP):
                        mm = pe.transpose(PT_BANK[:, k * P:(k + 1) * P], pr[:, s % 2, k * P:(k + 1) * P], ident)
                    mm.then_inc(pT_mm, 1)

            def transpose_qk(g, s):
                U = UPG * g + s
                prev = has_group(g, 1)
                if alive(g, s, 1):
                    pe.wait_ge(qn_done, past(U))
                    if alive(g, s, 3):
                        pe.wait_ge(oT_ev, past(U - 2))
                    else:
                        pe.wait_ge(qT_ev, past(U - 1))
                    for k in range(HP):
                        mm = pe.transpose(QT_BANK[:, k * P:(k + 1) * P], qkn[:, (s - 1) % 2, k * P:(k + 1) * P], ident)
                    mm.then_inc(qT_mm, 1)
                    pe.wait_ge(kn_done, past(U))
                    pe.wait_ge(kT_ev, past(2 * (U - 1)))
                    if prev and s == 7:
                        pe.wait_ge(u_done, ahead(3 * g - 2))
                    for k in range(HP):
                        mm = pe.transpose(KT_BANK[:, k * P:(k + 1) * P],
                                          qkn[:, (s - 1) % 2, UW + k * P:UW + (k + 1) * P], ident)
                    mm.then_inc(kT_mm, 1)

            def attend(g, s):
                U = UPG * g + s
                if alive(g, s, 2):
                    gv = g if s >= 2 else g - 1
                    sv = (s - 2) % UPG
                    pe.wait_ge(pT_ev, past(U - 1))
                    pe.wait_ge(vw_dma[sv % 2], vw_count(gv, sv))
                    pe.wait_ge(o_done, past(U - 2))
                    for k in range(HP):
                        for w in range(NW):
                            mm = pe.matmul(heads(PV_BANK[WIN * w:WIN * (w + 1), k * P:(k + 1) * P]),
                                           pT[:, s % 2, k, WIN * w:WIN * (w + 1)],
                                           vw[:, sv % 2, w, :, k * DH:(k + 1) * DH], start=True, stop=True,
                                           tile_position=(0, WIN * w))
                    mm.then_inc(pv_mm, 1)

            def body(g):
                own, prev = has_group(g, 0), has_group(g, 1)
                for s in range(UPG):
                    U = UPG * g + s
                    t, half = s // HALVES, s % HALVES
                    if own:
                        if s == 0:
                            pe.wait_ge(xsT_ev, g + 1)
                            pe.wait_ge(w_dma, past(16 * 2 * (g + 1)))
                        for i in range(2 if s < 7 else 0):
                            project(g, s, i)
                    if prev and s == 7:
                        take_turn(g, "a1")
                        pe.matmul(SHARED[:, :], w1[:, P:2 * P], xnT[:, :], start=True, stop=True).then_inc(turn_mm, 1)
                    if s == 7:
                        transpose_p(g, s)
                        transpose_o(g, s)
                        attend(g, s)
                        transpose_qk(g, s)
                    else:
                        transpose_o(g, s)
                        if own:
                            project(g, s, 2)
                        transpose_p(g, s)
                        transpose_qk(g, s)
                        attend(g, s)
                    if s % 2 == 1 and alive(g, s, 4):
                        tile = (s - 4) // 2 % TPG
                        gy = g if s >= 4 else g - 1
                        name = f"y{tile}"
                        take_turn(g, name)
                        pe.wait_ge(oT_ev, past(U - 3))
                        for k in range(INNER // P):
                            mm = pe.matmul(SHARED[:, 0:C], oT[:, tile % 2, k, :], wo[:, (gy // B) % 2, k, :],
                                           start=(k == 0), stop=(k == INNER // P - 1))
                        mm.then_inc(turn_mm, 1)
                    if prev and s == 7:
                        pe.wait_ge(kT_ev, past(2 * U if own else 2 * UNITS))
                        pe.wait_ge(u_done, ahead(3 * g - 2))
                        pe.matmul(KT_BANK[:, :], w1[:, 2 * P:3 * P], xnT[:, :], start=True, stop=True).then_inc(a_mm, 1)
                    if alive(g, s, 1):
                        sk = (s - 1) % UPG
                        tk, hk = sk // HALVES, sk % HALVES
                        pe.wait_ge(qT_ev, past(U))
                        pe.wait_ge(kT_ev, past(2 * U))
                        pe.wait_ge(sub_done, past(U - 1))
                        pe.matmul(heads(SC_BANK[:, :]), ident_b[:, :],
                                  mask_b[:, min(tk, 1), :].unsqueeze(1).to_broadcast([P, HU, 2 * WIN]),
                                  start=True, stop=True)
                        for k in range(HP):
                            for w in range(NW):
                                c0 = P * tk + WIN * w
                                mm = pe.matmul(heads(SC_BANK[WIN * w:WIN * (w + 1), k * P:(k + 1) * P]),
                                               qT[:, sk % 2, k, WIN * w:WIN * (w + 1)],
                                               kB[:, HP * hk + k, :, c0:c0 + 2 * WIN],
                                               start=False, stop=True, tile_position=(0, WIN * w),
                                               skip_group_check=True)
                        mm.then_inc(score_mm, 1)
                    if own and s == 2:
                        take_turn(g, "shift_att")
                        b = (g + 1) % B
                        shift(lambda a, n: x[:, bass.ds(TPG * b + a, n), 64:C], turn_mm)
                    if prev and s == 4:
                        take_turn(g, "shift_ffn")
                        pe.wait_ge(att_res, past(TPG * g))
                        b = (g + B - 1) % B
                        shift(lambda a, n: x[:, bass.ds(TPG * b + a, n), 64:C], turn_mm)
                    if own and s == 6:
                        project(g, 7, 0)
                    if prev and s == 6:
                        take_turn(g, "ln_t")
                        pe.wait_ge(f_xn, ahead(TPG * g))
                        for t_ in range(TPG):
                            mm = pe.transpose(SHARED[:, t_ * P:(t_ + 1) * P], xn[:, t_, :], ident)
                        mm.then_inc(turn_mm, 1)
                    if own and s == 6:
                        project(g, 7, 1)
                        project(g, 7, 2)
                    if prev and s == 6:
                        pe.wait_ge(xnT_done, past(g))
                        pe.wait_ge(w1_dma, past(16 * g))
                        gate = lambda i: w1[:, DFF + i * P:DFF + (i + 1) * P]
                        take_turn(g, "gate0")
                        pe.matmul(SHARED[:, :], gate(0), xnT[:, :], start=True, stop=True).then_inc(turn_mm, 1)
                        if own:
                            pe.wait_ge(qT_ev, past(U))
                        else:
                            pe.wait_ge(oT_ev, UNITS)
                        pe.matmul(QT_BANK[:, :], gate(1), xnT[:, :], start=True, stop=True).then_inc(gate_mm, 1)
                        pe.wait_ge(pT_ev, past(U - 1 if own else UNITS))
                        pe.wait_ge(w1_pad, 1)
                        pe.matmul(PT_BANK[:, :], gate(2), xnT[:, :], start=True, stop=True).then_inc(gate_mm, 1)
                        pe.wait_ge(kT_ev, past(2 * U if own else 2 * UNITS))
                        pe.matmul(KT_BANK[:, :], w1[:, 0:P], xnT[:, :], start=True, stop=True).then_inc(a_mm, 1)
                    if own and s == 7:
                        take_turn(g, "x_t")
                        pe.wait_ge(xa_low, g + 1)
                        x_transposes(turn_mm)
                    if prev and s == 7:
                        if own:
                            pe.wait_ge(pT_ev, past(U - 1))
                        else:
                            pe.wait_ge(gate_read, past(2 * g))
                        pe.wait_ge(u_done, ahead(3 * g))
                        pe.wait_ge(w2_dma, past(32 * g))
                        for t_ in range(TPG):
                            for i, (r, m) in enumerate(BLK):
                                mm = pe.matmul(PT_BANK[:, t_ * P:(t_ + 1) * P], uT[0:m, i, t_ * P:(t_ + 1) * P],
                                               w2[0:m, i, :], start=(i == 0), stop=(i == len(BLK) - 1))
                        mm.then_inc(down_mm, 1)

            body(0)
            with pe.Fori(1, GROUPS) as g:
                body(g)
            body(GROUPS)

        @block.scalar
        def _(act):
            act.wait_ge(wxT_mm, 1)
            act.activation(wxT[:, :, :].rearrange("p a c -> p (a c)"), ps[0][:, :], ACT.Copy).then_inc(wxT_ev, 1)
            act.wait_ge(ctxT_mm, 1)
            act.activation(ctxT[:, :, :].rearrange("p b s -> p (b s)"), ps[1][:, 0:B * CTX], ACT.Copy).then_inc(ctxT_ev, 1)
            act.wait_ge(small_dma, 16 * 6)
            act.activation(tg[:, :], gcol[:, :], ACT.Tanh).then_inc(tanh_ready, 1)
            act.wait_ge(kx_mm, 1)
            act.activation(kxT[:, :, :].rearrange("p b s -> p (b s)"), ps[2][:, 0:B * CTX], ACT.Identity,
                           bias=bcol[:, 1:2]).then_inc(kx_ev, 1)
            act.wait_ge(vx_mm, 1)
            act.activation(vx[:, :, :].rearrange("p b c -> p (b c)"), ps[3][0:CTX, :], ACT.Copy).then_inc(vx_ev, 1)
            with act.Fori(0, B // 2) as pair:
                for j in range(2):
                    act.wait_ge(a_xnT, 2 * pair + j + 1)
                    act.activation(xnT_x[j], ps[4 * j][:, :], ACT.Copy).then_inc(a_xnTev, 1)
                for j in range(2):
                    act.wait_ge(a_q, 2 * pair + j + 1)
                    act.activation(q_x[j], ps[4 * j + 1][:, :], ACT.Identity, bias=bcol[:, 0:1]).then_inc(a_qev, 1)
                for j in range(2):
                    act.wait_ge(a_sub, 2 * pair + j + 1)
                    act.activation(pr_x[j], pr_x[j], ACT.Exp, scale=float(C) ** -0.5).then_inc(a_exp, 1)
                for j in range(2):
                    act.wait_ge(a_pT, 2 * pair + j + 1)
                    act.activation(pT_x[j][0:CTX, :], ps[4 * j + 3][0:CTX, :], ACT.Copy).then_inc(a_pTev, 1)
                for j in range(2):
                    act.wait_ge(a_rT, 2 * pair + j + 1)
                    act.activation(rT_x[j], ps[4 * j + 1][:, :], ACT.Copy).then_inc(a_rTev, 1)
            act.preload_act_table_set("natural_log_exp_and_others")
            act.wait_ge(b_x, ahead(B * TPG))
            act.activation(xa[:, :, 0:64], x[:, 0:TPG, 0:64], ACT.Copy).then_inc(p_low, 1)
            act.wait_ge(p_xT, 1)
            act.activation(xsT[:, :], SHARED[:, :], ACT.Copy).then_inc(xsT_ev, 1)
            act.wait_ge(zero_ready, 2)
            act.wait_ge(cst_ready, 5)

            def copy_out(g, s, i):
                U = UPG * g + s
                act.wait_ge(sq_done, past(U - 1))
                act.wait_ge(cos_done, past(2 * (U - 1)))
                act.wait_ge(sin_done, past(2 * (U - 1)))
                act.wait_ge(qkv_mm, 3 * U + i + 1)
                act.activation(qk[:, s % 2, i * UW:(i + 1) * UW], QKV_BANKS[(3 * s + i) % 2][:, :],
                               ACT.Copy).then_inc(qkv_ev, 1)

            def exponentials(g, s):
                U = UPG * g + s
                if alive(g, s, 2):
                    act.wait_ge(sub_done, past(U - 1))
                    act.wait_ge(pT_mm, past(U - 3))
                    act.wait_ge(sum_done, past(U - 3))
                    act.activation(pr[:, s % 2, :], pr[:, s % 2, :], ACT.Exp).then_inc(exp_done, 1)

            def estimate(U):
                act.wait_ge(ssm_done, past(U))
                act.wait_ge(newton_done, past(2 * (U - 1)))
                act.activation(lnn[:, :], ssm[:, :], ACT.Ln, scale=LN_SHIFT).then_inc(ln_done, 1)
                act.wait_ge(ln_done, past(U))
                act.wait_ge(rn_done, past(U - 1))
                act.activation(seed[:, :], lnn[:, :], ACT.Exp, bias=shift_back[:, 0:1], scale=-0.5).then_inc(seed_done, 1)

            def copy_pT(g, s):
                U = UPG * g + s
                if alive(g, s, 2):
                    act.wait_ge(pT_mm, past(U - 1))
                    act.wait_ge(pv_mm, past(U - 3))
                    act.activation(pT[:, s % 2].rearrange("p k q -> p (k q)"), PT_BANK[:, :],
                                   ACT.Copy).then_inc(pT_ev, 1)

            def body(g):
                own, prev = has_group(g, 0), has_group(g, 1)
                for s in range(UPG):
                    U = UPG * g + s
                    if own:
                        if s % 2 == 0 and s > 0:
                            estimate(U)
                        if s < 7:
                            copy_out(g, s, 0)
                    if s == 7:
                        copy_pT(g, s)
                    if alive(g, s, 1) and s % 2 == 1:
                        estimate(U)
                    if 0 < s < 7:
                        exponentials(g, s)
                    if own and s == 3:
                        act.wait_ge(turn_mm, turn(g, "shift_att"))
                        act.activation(xa[:, :, 64:C], heads(SHARED[:, 0:TPG * 64]), ACT.Copy).then_inc(turn_read, 1)
                    if prev and s == 5:
                        act.wait_ge(f_xn, ahead(TPG * (g - 1)))
                        act.wait_ge(turn_mm, turn(g, "shift_ffn"))
                        act.activation(xf[:, :, 64:C], heads(SHARED[:, 0:TPG * 64]), ACT.Copy).then_inc(turn_read, 1)
                    if alive(g, s, 3):
                        so = (s - 3) % UPG
                        to, ho = so // HALVES, so % HALVES
                        act.wait_ge(oT_mm, past(U - 2))
                        if alive(g, s, 3 + 2 * HALVES + ho):
                            act.wait_ge(att_res, past(TPG * g + (s - 3) // HALVES - 1))
                        act.activation(oT[:, to % 2, HP * ho:HP * ho + HP, :].rearrange("p k q -> p (k q)"),
                                       QT_BANK[:, :], ACT.Copy).then_inc(oT_ev, 1)
                    if own and s < 7:
                        copy_out(g, s, 1)
                    if s < 7:
                        copy_pT(g, s)
                    if alive(g, s, 1):
                        sk = (s - 1) % UPG
                        tk, hk = sk // HALVES, sk % HALVES
                        act.wait_ge(qT_mm, past(U))
                        act.wait_ge(score_mm, past(U - 2))
                        act.activation(qT[:, sk % 2].rearrange("p k q -> p (k q)"), QT_BANK[:, :],
                                       ACT.Copy).then_inc(qT_ev, 1)
                    if prev and s == 6:
                        act.wait_ge(f_var, past(g))
                        act.activation(f_tmp[:, :], vare[:, :], ACT.Ln).then_inc(f_ln, 1)
                        act.wait_ge(f_ln, past(g))
                        act.activation(f_seed[:, :], f_tmp[:, :], ACT.Exp, scale=-0.5).then_inc(f_seeded, 1)
                    if alive(g, s, 1):
                        act.wait_ge(kT_mm, past(U))
                        act.wait_ge(score_mm, past(U - 6))
                        for h in range(2):
                            act.activation(kB[64 * h:64 * h + 64, HP * hk:HP * hk + HP, h, WIN + P * tk:WIN + P * tk + P],
                                           KT_BANK[64 * h:64 * h + 64, :].rearrange("p (k q) -> p k q", q=P),
                                           ACT.Copy).then_inc(kT_ev, 1)
                    if own:
                        act.wait_ge(qkv_ev, 3 * U + 2)
                        act.wait_ge(ss_done, past(U))
                        act.activation(sq[:, :], qk[:, s % 2, :], ACT.Square).then_inc(sq_done, 1)
                    if own:
                        act.wait_ge(qkv_mm, 3 * U + 3)
                        if alive(g, s, 2):
                            s2, g2 = (s - 2) % UPG, (g if s >= 2 else g - 1)
                            act.wait_ge(vw_dma[s2 % 2], vw_count(g2, s2))
                        act.activation(vs[:, s % 4], QKV_BANKS[(3 * s + 2) % 2][:, :].rearrange(
                            "p (k h d) -> p h k d", h=2, d=DH), ACT.Copy).then_inc(qkv_ev, 1)
                    if own and s == 3:
                        act.wait_ge(turn_mm, turn(g, "shift_att"))
                        b = (g + 1) % B
                        src = x[:, bass.ds(TPG * b, TPG), 0:64]
                        act.activation(xa[:, :, 0:64], src, ACT.Copy).then_inc(xa_low, 1)
                    if prev and s == 4:
                        act.wait_ge(att_res, past(TPG * g))
                        b = (g + B - 1) % B
                        src = x[:, bass.ds(TPG * b, TPG), 0:64]
                        act.activation(xf[:, :, 0:64], src, ACT.Copy).then_inc(xf_low, 1)
                    if own and s == 6:
                        copy_out(g, 7, 0)
                    if prev and s == 6:
                        act.wait_ge(turn_mm, turn(g, "ln_t"))
                        act.wait_ge(cur_done, past(g))
                        act.activation(xnT[:, :], SHARED[:, :], ACT.Identity, bias=cur[:, 1:2],
                                       scale=cur[:, 0:1]).then_inc(turn_read, 1)
                        act.wait_ge(turn_read, turn(g, "ln_t"))
                        act.sem_inc(xnT_done, 1)
                    if own and s == 6:
                        exponentials(g, 7)
                        copy_out(g, 7, 1)
                    if prev and s == 6:
                        act.preload_act_table(ACT.Gelu)
                        act.wait_ge(cur_done, past(g))
                        act.wait_ge(turn_mm, turn(g, "gate0"))
                        act.activation(uT[:, 0, :], SHARED[:, :], ACT.Gelu, bias=cur[:, 5:6]).then_inc(turn_read, 1)
                        for i, bank in ((1, QT_BANK), (2, PT_BANK)):
                            m = BLK[i][1]
                            act.wait_ge(gate_mm, past(2 * g - 2 + i))
                            act.activation(uT[0:m, i, :], bank[0:m, :], ACT.Gelu,
                                           bias=cur[0:m, 5 + i:6 + i]).then_inc(gate_read, 1)
                        act.preload_act_table_set("natural_log_exp_and_others")
                    if own and s == 7:
                        estimate(U + 1)
                        act.wait_ge(turn_mm, turn(g, "x_t"))
                        act.wait_ge(qkv_mm, 3 * U + 3)
                        act.activation(xsT[:, :], SHARED[:, :], ACT.Copy).then_inc(turn_read, 1)
                        act.wait_ge(turn_read, turn(g, "x_t"))
                        act.sem_inc(xsT_ev, 1)
                        exponentials(g + 1, 0)

            body(0)
            with act.Fori(1, GROUPS) as g:
                body(g)
            body(GROUPS)

        @block.vector
        def _(dve):
            for start in (f_xn, f_rstd, u_done, b_x, down_read):
                dve.sem_inc(start, 1)
            dve.memset(ones[:, :], 1.0).then_inc(cst_ready, 1)
            dve.memset(minus_half[:, :], -0.5).then_inc(cst_ready, 1)
            dve.memset(shift_back[:, :], 0.5 * float(np.log(LN_SHIFT))).then_inc(cst_ready, 1)
            dve.wait_ge(mats_dma, 16 * 2)
            dve.tensor_copy(mask_b[:, :, :], mask_f[:, :, :]).then_inc(cst_ready, 1)
            dve.tensor_copy(ident_b[:, :], ident).then_inc(cst_ready, 1)

            with dve.Fori(0, B // 2) as pair:
                def normalise(src, dst, stat, rst, done):
                    settle(dve)
                    for j in range(2):
                        b = 2 * pair + j
                        for t in range(TPG):
                            dve.bn_stats(stats_x[j][:, t, :], src(b, j, t)).then_inc(stat, 1)
                        dve.wait_ge(stat, 2 * TPG * b + TPG)
                        settle(dve)
                        for t in range(TPG):
                            dve.bn_aggr(mv_x[j][:, t, :], stats_x[j][:, t, :]).then_inc(stat, 1)
                    for j in range(2):
                        b = 2 * pair + j
                        dve.wait_ge(rst, 2 * b + 2)
                        dve.wait_ge(stat, 2 * TPG * b + 2 * TPG)
                        for t in range(TPG):
                            dve.tensor_scalar(dst(b, j, t), src(b, j, t), mv_x[j][:, t, 0:1], rstd_x[j][:, t:t + 1],
                                              ALU.subtract, ALU.mult).then_inc(done, 1)

                dve.wait_ge(x_dma, 16 * pair + 16)
                dve.wait_ge(b_x, ahead(2 * TPG * pair))
                normalise(lambda b, j, t: x1[:, TPG * b + t, :], lambda b, j, t: xn_x[j][:, t, :], a_stat, a_rstd, a_xn)
                for j in range(2):
                    b = 2 * pair + j
                    dve.wait_ge(a_sc, b + 1)
                    sc = heads(ps[4 * j + 2][:, :], P)[:, :, 0:CTX]
                    dve.tensor_reduce(mx_x[j], sc, AX.X, ALU.max).then_inc(a_mx, 1)
                    dve.wait_ge(a_mx, b + 1)
                    dve.tensor_tensor(pr_x[j], sc, spread(mx_x[j], CTX), ALU.subtract).then_inc(a_sub, 1)
                for j in range(2):
                    b = 2 * pair + j
                    dve.wait_ge(a_exp, b + 1)
                    dve.tensor_reduce(rs_x[j], pr_x[j], AX.X, ALU.add).then_inc(a_sum, 1)
                    dve.wait_ge(a_sum, b + 1)
                    dve.reciprocal(rr_x[j], rs_x[j]).then_inc(a_rec, 1)
                    dve.wait_ge(a_rec, b + 1)
                    dve.tensor_tensor(pr_x[j], pr_x[j], spread(rr_x[j], CTX), ALU.mult).then_inc(a_pn, 1)
                for j in range(2):
                    b = 2 * pair + j
                    dve.wait_ge(a_att, b + 1)
                    dve.wait_ge(a_xn, 4 * b + 4)
                    dve.tensor_tensor(res_x[j], heads(ps[4 * j][:, :], P), xn_x[j], ALU.add).then_inc(a_res, 1)
                for j in range(2):
                    b = 2 * pair + j
                    rows = x1[:, bass.ds(TPG * b, TPG), :]
                    dve.wait_ge(tanh_ready, 1)
                    dve.wait_ge(a_y, b + 1)
                    dve.scalar_tensor_tensor(out=rows, in0=heads(ps[4 * j + 2][:, :], P), scalar=tg[:, 0:1],
                                             in1=rows, op0=ALU.mult, op1=ALU.add).then_inc(a_x1, 1)
                dve.wait_ge(a_x1, 2 * pair + 2)
                normalise(lambda b, j, t: x1[:, TPG * b + t, :], lambda b, j, t: x[:, TPG * b + t, :], b_stat, b_rstd, b_x)
            dve.wait_ge(p_shift, 1)
            dve.tensor_copy(xa[:, :, 64:C], heads(SHARED[:, 0:TPG * 64])).then_inc(p_up, 1)

            def norms(g, s, U):
                dve.wait_ge(seed_done, past(U))
                dve.scalar_tensor_tensor(out=step[:, :], in0=seed[:, :], scalar=-0.5, in1=seed[:, :],
                                         op0=ALU.mult, op1=ALU.mult).then_inc(newton_done, 1)
                dve.wait_ge(newton_done, past(2 * U - 1))
                dve.tensor_tensor(step[:, :], step[:, :], ssm[:, :], ALU.mult).then_inc(newton_done, 1)
                dve.wait_ge(newton_done, past(2 * U))
                dve.wait_ge(kn_done, past(U - 1))
                dve.scalar_tensor_tensor(out=rn[:, :], in0=step[:, :], scalar=1.5, in1=seed[:, :],
                                         op0=ALU.add, op1=ALU.mult).then_inc(rn_done, 1)

            def scale_q(g, s, U):
                dve.wait_ge(rn_done, past(U))
                dve.wait_ge(rotq_done, past(U))
                q = heads(qkn[:, (s - 1) % 2, 0:UW])
                dve.tensor_tensor(q, q, spread(rn[:, 0:HU], DH), ALU.mult).then_inc(qn_done, 1)

            def less_maxima(g, s):
                U = UPG * g + s
                dve.wait_ge(score_mm, past(U - 1))
                dve.wait_ge(sub_done, past(U - 2))
                dve.tensor_reduce(mx[:, :], heads(SC_BANK[:, :]), AX.X, ALU.max).then_inc(max_done, 1)
                dve.wait_ge(max_done, past(U - 1))
                dve.wait_ge(exp_done, past(U - 3))
                dve.tensor_tensor(heads(pr[:, s % 2, :]), heads(SC_BANK[:, :]), spread(mx[:, :], DH),
                                  ALU.subtract).then_inc(sub_done, 1)

            def head(g, s):
                U = UPG * g + s
                if s % 2 == 0 and alive(g, s, 1):
                    norms(g, s, U)
                if alive(g, s, 2) and s < 7:
                    less_maxima(g, s)
                if s % 2 == 1 and alive(g, s, 1):
                    norms(g, s, U)
                if alive(g, s, 1):
                    scale_q(g, s, U)

            def body(g):
                own, prev = has_group(g, 0), has_group(g, 1)
                for s in range(UPG):
                    U = UPG * g + s
                    if prev and s == 7:
                        dve.wait_ge(a_mm, past(2 * g - 1))
                        dve.wait_ge(turn_read, turn(g, "gate0"))
                        dve.scalar_tensor_tensor(out=uT[:, 0, :], in0=KT_BANK[:, :], scalar=cur[:, 2:3],
                                                 in1=uT[:, 0, :], op0=ALU.add, op1=ALU.mult).then_inc(u_done, 1)
                    if prev and s == 7:
                        dve.wait_ge(turn_mm, turn(g, "a1"))
                        dve.wait_ge(gate_read, past(2 * g - 1))
                        dve.scalar_tensor_tensor(out=uT[:, 1, :], in0=SHARED[:, :], scalar=cur[:, 3:4],
                                                 in1=uT[:, 1, :], op0=ALU.add, op1=ALU.mult).then_inc(turn_read, 1)
                        dve.wait_ge(turn_read, turn(g, "a1"))
                        dve.sem_inc(u_done, 1)
                    if s > 0:
                        head(g, s)
                    if prev and s == 6:
                        dve.wait_ge(f_xn, ahead(TPG * (g - 1)))
                        dve.wait_ge(turn_read, turn(g, "shift_ffn"))
                        dve.wait_ge(xf_low, past(g))
                        settle(dve)
                        for t_ in range(TPG):
                            dve.bn_stats(stats[:, t_, :], xf[:, t_, :]).then_inc(f_stat, 1)
                        dve.wait_ge(f_stat, past(TPG * g))
                        settle(dve)
                        for t_ in range(TPG):
                            dve.bn_aggr(mv[:, t_, :], stats[:, t_, :]).then_inc(f_aggr, 1)
                        dve.wait_ge(f_aggr, past(TPG * g))
                        dve.tensor_scalar(vare[:, :], mv[:, :, 1], LN_EPS, None, ALU.add).then_inc(f_var, 1)
                    if own:
                        t = s // HALVES
                        if s == 0:
                            dve.wait_ge(table_ready, TPG + g)
                        dve.wait_ge(rotq_done, past(U))
                        dve.wait_ge(rotk_done, past(U))
                        for i in range(2):
                            dve.wait_ge(qkv_ev, 3 * U + i + 1)
                            table = tables[:, (g // B) % 2, t, 2 * DH * i:2 * DH * i + DH]
                            cut = slice(i * UW, (i + 1) * UW)
                            dve.tensor_tensor(heads(ra[:, cut]), heads(qk[:, s % 2, cut]),
                                              table.unsqueeze(1).to_broadcast([P, HU, DH]),
                                              ALU.mult).then_inc(cos_done, 1)
                    if alive(g, s, 2):
                        dve.wait_ge(rec_done, past(U - 2))
                        dve.wait_ge(exp_done, past(U - 1))
                        dve.tensor_reduce(rs[:, :], heads(pr[:, s % 2, :]), AX.X, ALU.add).then_inc(sum_done, 1)
                        dve.wait_ge(sum_done, past(U - 1))
                        dve.reciprocal(rr[:, s % 2, :], rs[:, :]).then_inc(rec_done, 1)
                    if own:
                        dve.wait_ge(sin_done, 2 * U + 1)
                        dve.wait_ge(cos_done, 2 * U + 1)
                        dve.wait_ge(kT_mm, past(U - 1))
                        dve.tensor_tensor(qkn[:, s % 2, 0:UW], ra[:, 0:UW], rb[:, 0:UW], ALU.add).then_inc(rotq_done, 1)
                    if prev and s == 6:
                        dve.wait_ge(f_seeded, past(g))
                        dve.scalar_tensor_tensor(out=f_tmp[:, :], in0=f_seed[:, :], scalar=-0.5, in1=f_seed[:, :],
                                                 op0=ALU.mult, op1=ALU.mult).then_inc(f_newton, 1)
                        dve.wait_ge(f_newton, past(2 * g - 1))
                        dve.tensor_tensor(f_tmp[:, :], f_tmp[:, :], vare[:, :], ALU.mult).then_inc(f_newton, 1)
                        dve.wait_ge(f_newton, past(2 * g))
                        dve.scalar_tensor_tensor(out=rstd[:, :], in0=f_tmp[:, :], scalar=1.5, in1=f_seed[:, :],
                                                 op0=ALU.add, op1=ALU.mult).then_inc(f_rstd, 1)
                        dve.wait_ge(f_rstd, ahead(g))
                        for t_ in range(TPG):
                            dve.tensor_scalar(xn[:, t_, :], xf[:, t_, :], mv[:, t_, 0:1], rstd[:, t_:t_ + 1],
                                              ALU.subtract, ALU.mult).then_inc(f_xn, 1)
                    if own and s == 6:
                        less_maxima(g, 7)
                    if alive(g, s, 2):
                        dve.wait_ge(rec_done, past(U - 1))
                        dve.wait_ge(pv_mm, past(U - 1))
                        dve.wait_ge(oT_mm, past(U - 2))
                        dve.tensor_tensor(heads(o[:, :]), heads(PV_BANK[:, :]), spread(rr[:, s % 2, :], DH),
                                          ALU.mult).then_inc(o_done, 1)
                    if own:
                        dve.wait_ge(sq_done, U + 1)
                        dve.tensor_reduce(ss[:, :], heads(sq[:, :]), AX.X, ALU.add).then_inc(ss_done, 1)
                        dve.wait_ge(rn_done, past(U))
                        dve.wait_ge(ss_done, U + 1)
                        dve.tensor_scalar(ssm[:, :], ss[:, :], NORM_MIN ** 2, None, ALU.max).then_inc(ssm_done, 1)
                    if s % 2 == 1 and alive(g, s, 4):
                        tile = (s - 4) // 2 % TPG
                        gy = g if s >= 4 else g + B - 1
                        row = x[:, TPG * (gy % B) + tile, :]
                        dve.wait_ge(turn_mm, turn(g, f"y{tile}"))
                        dve.wait_ge(turn_read, past(turn(g, f"y{tile}") - 1))
                        dve.tensor_tensor(row, row, SHARED[:, 0:C], ALU.add).then_inc(turn_read, 1)
                        dve.wait_ge(turn_read, turn(g, f"y{tile}"))
                        dve.sem_inc(att_res, 1)
                    if prev and s == 7:
                        m = BLK[2][1]
                        dve.wait_ge(a_mm, past(2 * g))
                        dve.wait_ge(gate_read, past(2 * g))
                        dve.scalar_tensor_tensor(out=uT[0:m, 2, :], in0=KT_BANK[0:m, :], scalar=cur[0:m, 4:5],
                                                 in1=uT[0:m, 2, :], op0=ALU.add, op1=ALU.mult).then_inc(u_done, 1)
                    if own and s == 7:
                        head(g + 1, 0)
                    if prev and s == 7:
                        b = (g + B - 1) % B
                        rows = x[:, bass.ds(TPG * b, TPG), :]
                        dve.wait_ge(down_mm, past(g))
                        dve.wait_ge(b2_done, past(g))
                        dve.tensor_tensor(rows, rows, heads(PT_BANK[:, :], C), ALU.add).then_inc(down_read, 1)

            body(0)
            with dve.Fori(1, GROUPS) as g:
                body(g)
            body(GROUPS)
            dve.wait_ge(down_read, ahead(GROUPS))
            for b in range(B):
                rows = lambda buf: buf[:, TPG * b:TPG * (b + 1), :].rearrange("p t c -> p (t c)")
                dve.scalar_tensor_tensor(out=rows(x1), in0=rows(x), scalar=tg[:, 1:2], in1=rows(x1),
                                         op0=ALU.mult, op1=ALU.add).then_inc(fin, 1)

        @block.gpsimd
        def _(pool):
            pool.memset(cols[:, :, :], 0.0).then_inc(zero_ready, 1)
            pool.memset(w1[:, 2 * DFF:], 0.0).then_inc(w1_pad, 1)
            pool.memset(kB[:, :, :, :], 0.0).then_inc(zero_ready, 1)
            pool.wait_ge(cst_ready, 3)

            with pool.Fori(0, B // 2) as pair:
                for stat, rst in ((a_stat, a_rstd), (b_stat, b_rstd)):
                    for j in range(2):
                        b = 2 * pair + j
                        pool.wait_ge(stat, 2 * TPG * b + 2 * TPG)
                        settle(pool)
                        pool.tensor_scalar(vare_x[j], mv_x[j][:, :, 1], LN_EPS, None, ALU.add).then_inc(rst, 1)
                        pool.wait_ge(rst, 2 * b + 1)
                        pool.tensor_tensor(rstd_x[j], vare_x[j], minus_half[:, 0:TPG], ALU.pow).then_inc(rst, 1)

            pool.wait_ge(cst_dma, 16 * 7)
            for t in range(TPG):
                pool.tensor_tensor(tables[:, 0, t, :], rope[:, t, :], scales[:, 0, :], ALU.mult).then_inc(table_ready, 1)
            pool.wait_ge(b_x, ahead(B * TPG))
            pool.memset(free, 0.0).then_inc(vw_zero, 1)

            def add_b2(g):
                pool.wait_ge(turn_mm, turn(g, "shift_ffn"))
                pool.wait_ge(xf_low, past(g))
                settle(pool)
                b = (g + B - 1) % B
                rows = x[:, bass.ds(TPG * b, TPG), :]
                pool.tensor_tensor(rows, rows, b2r[:, (g - 1) // B, :].unsqueeze(1).to_broadcast([P, TPG, C]),
                                   ALU.add).then_inc(b2_done, 1)

            def body(g):
                own, prev = has_group(g, 0), has_group(g, 1)
                for s in range(UPG):
                    U = UPG * g + s
                    if own:
                        t = s // HALVES
                        if s == 0:
                            pool.wait_ge(table_ready, TPG + g)
                        for i in range(2):
                            pool.wait_ge(qkv_ev, 3 * U + i + 1)
                            pool.wait_ge(rotq_done, past(U))
                            pool.wait_ge(rotk_done, past(U))
                            settle(pool)
                            table = tables[:, (g // B) % 2, t, 2 * DH * i + DH:2 * DH * (i + 1)]
                            cut = slice(i * UW, (i + 1) * UW)
                            halves = lambda ap: ap.rearrange("p (h a d) -> p h a d", a=2, d=DH // 2)
                            pool.tensor_tensor(
                                halves(rb[:, cut]), halves(qk[:, s % 2, cut])[:, :, ::-1, :],
                                table.rearrange("p (a d) -> p a d", a=2).unsqueeze(1).to_broadcast([P, HU, 2, DH // 2]),
                                ALU.mult).then_inc(sin_done, 1)
                        pool.wait_ge(cos_done, 2 * U + 2)
                        pool.wait_ge(sin_done, 2 * U + 2)
                        pool.wait_ge(kT_mm, past(U - 1))
                        settle(pool)
                        pool.tensor_tensor(qkn[:, s % 2, UW:], ra[:, UW:], rb[:, UW:], ALU.add).then_inc(rotk_done, 1)
                        if prev and s == 5:
                            add_b2(g)
                        pool.wait_ge(rotk_done, U + 1)
                        pool.wait_ge(rn_done, U + 1)
                        settle(pool)
                        k = heads(qkn[:, s % 2, UW:])
                        pool.tensor_tensor(k, k, spread(rn[:, HU:], DH), ALU.mult).then_inc(kn_done, 1)
                    if prev and s == 4:
                        if isinstance(g, int):
                            pool.wait_ge(cols_dma, 16 * 9)
                        pool.wait_ge(u_done, ahead(3 * (g - 1)))
                        pool.tensor_copy(cur[:, :], cols[:, (g - 1) // B, :]).then_inc(cur_done, 1)
                    if prev and not own and s == 5:
                        add_b2(g)
                    if own and s == 7:
                        layer, place, part = (g // B + 1) % DEPTH, (g // B + 1) % 2, g % B
                        pool.wait_ge(cos_done, past(2 * UPG * g))
                        settle(pool)
                        pool.tensor_tensor(tables[:, place, part, :], rope[:, part, :], scales[:, layer, :],
                                           ALU.mult).then_inc(table_ready, 1)

            pool.wait_ge(cols_dma, 16 * 9)
            body(0)
            with pool.Fori(1, GROUPS) as g:
                body(g)
            body(GROUPS)


_INS = ["x", "ctx_1024", "g_xattn", "g_ffn", "L0_xattn_Wq", "L0_xattn_bq", "L0_xattn_Wk", "L0_xattn_bk", "L0_xattn_Wv",
        "L0_xattn_bv", "L0_xattn_Wo", "L0_xattn_bo", "L0_ffn_Wqkv", "L0_ffn_q_scale", "L0_ffn_k_scale", "L0_ffn_Wo",
        "L0_ffn_ln_g", "L0_ffn_ln_b", "L0_ffn_W1", "L0_ffn_b1", "L0_ffn_W2", "L0_ffn_b2"]


def kernel(**inputs):
    import numpy as _np
    import concourse.bacc as _bacc
    from concourse import mybir as _mybir
    from concourse.bass_utils import run_bass_kernel_spmd as _run

    nc = _bacc.Bacc("TRN2", target_bir_lowering=False, num_devices=1)
    arrays, args = {}, []
    given = [(n, _np.ascontiguousarray(inputs[n])) for n in _INS]
    given += list(zip(("rope", "mats", "mask"), constants()))
    for name, a in given:
        arrays[f"in_{name}_dram"] = a
        args.append(nc.dram_tensor(f"in_{name}_dram", a.shape, _mybir.dt.from_np(a.dtype), kind="ExternalInput").ap())
    out = nc.dram_tensor("out_0_dram", (B, N, C), _mybir.dt.float32, kind="ExternalOutput").ap()
    build(nc, *args, out)
    r = _run(nc, [arrays], core_ids=[0])
    return r.results[0]["out_0_dram"]
```
